# Optimizing a Trainium2 kernel written in Bass

```python
import numpy as np
import jax
import jax.numpy as jnp

def _softmax(x, axis=-1):
    return jax.nn.softmax(x, axis=axis)

def _gelu(x):
    return jax.nn.gelu(x, approximate=True)

def _silu(x):
    return jax.nn.silu(x)

def _sigmoid(x):
    return jax.nn.sigmoid(x)

def _layernorm(x, axis=-1, eps=1e-05):
    m = jnp.mean(x, axis=axis, keepdims=True)
    v = jnp.var(x, axis=axis, keepdims=True)
    return (x - m) / jnp.sqrt(v + eps)

def _scatter_add(tgt, idx, src, axis=0):
    return tgt.at[idx].add(src)

def _segment_sum(src, seg, n):
    return jax.ops.segment_sum(src, seg, n)
kernel_name = 'mk_adaln_attn_ffn_d1_seqx_r4_cca5c3'

def setup_inputs(seed: int=0):
    np.random.seed(seed)
    _w = jnp.asarray

    def _rec_inputs():
        import jax
        import jax.numpy as jnp
        _rk = jax.random.key(seed)
        x = -0.000125 + 0.9999 * jax.random.normal(jax.random.fold_in(_rk, 1), (32, 64, 1024), jnp.float32)
        _lenS = 64 - jax.random.randint(jax.random.fold_in(_rk, 7), (32,), 0, max(1, 64 // 4) + 1, jnp.int32)
        _lenS2 = 64 - jax.random.randint(jax.random.fold_in(_rk, 8), (32,), 0, max(1, 64 // 4) + 1, jnp.int32)
        cond_128 = 0.0061147 + 1.02565 * jax.random.normal(jax.random.fold_in(_rk, 11), (32, 128), jnp.float32)
        fside_S_0 = -0.022604 + 0.987366 * jax.random.normal(jax.random.fold_in(_rk, 12), (64,), jnp.float32)
        return (x, cond_128, fside_S_0)
    x, cond_128, fside_S_0 = _rec_inputs()

    def _L0_cond_setup():
        import jax, jax.numpy as jnp
        import numpy as np
        K = 8
        T = 1.0
        D_EMBD = 128
        IN_C = 64
        OUT_C = 64
        BS = 32
        H = 1024
        HID = 128
        key = jax.random.key(seed)
        ks = jax.random.split(key, 10)
        s = lambda fan_in: 1.0 / np.sqrt(fan_in)
        return {'x': jax.random.normal(ks[0], (BS, IN_C, H), dtype=jnp.float32), 'embedding': jax.random.normal(ks[1], (BS, D_EMBD), dtype=jnp.float32), 'W0': jax.random.normal(ks[2], (D_EMBD, HID), dtype=jnp.float32) * s(D_EMBD), 'b0': jnp.zeros((HID,), dtype=jnp.float32), 'W1': jax.random.normal(ks[3], (HID, HID), dtype=jnp.float32) * s(HID), 'b1': jnp.zeros((HID,), dtype=jnp.float32), 'W2': jax.random.normal(ks[4], (HID, K), dtype=jnp.float32) * s(HID), 'b2': jnp.zeros((K,), dtype=jnp.float32), 'weight': jax.random.normal(ks[5], (K, OUT_C, IN_C, 1), dtype=jnp.float32) * s(IN_C), 'bias_k': jax.random.normal(ks[6], (K, OUT_C), dtype=jnp.float32) * 0.1}
    _L0_cond_all = _L0_cond_setup()
    _L0_cond_in = {k: v for k, v in _L0_cond_all.items() if k in ('W0', 'b0', 'W1', 'b1', 'W2', 'b2', 'weight', 'bias_k')}
    del _L0_cond_all

    def _L0_attn_setup():
        import jax, jax.numpy as jnp
        import numpy as np
        HDC_DIM = 1024
        N_HEADS = 4
        HEAD_DIM = HDC_DIM // N_HEADS

        def _ste_sign(w):
            alpha = jnp.mean(jnp.abs(w), axis=-1, keepdims=True)
            hard = alpha * jnp.sign(w)
            hard = jnp.where(hard == 0, alpha, hard)
            return jax.lax.stop_gradient(hard - w) + w
        key = jax.random.key(seed)
        kx, kq, kk, kv = jax.random.split(key, 4)
        B, T = (4, 512)
        x = jax.random.normal(kx, (B, T, HDC_DIM), dtype=jnp.float32)
        bv_q = jax.random.normal(kq, (N_HEADS, HEAD_DIM), dtype=jnp.float32) * 0.02
        bv_k = jax.random.normal(kk, (N_HEADS, HEAD_DIM), dtype=jnp.float32) * 0.02
        bv_v = jax.random.normal(kv, (N_HEADS, HEAD_DIM), dtype=jnp.float32) * 0.02
        return {'x': x, 'bv_q': bv_q, 'bv_k': bv_k, 'bv_v': bv_v}
    _L0_attn_all = _L0_attn_setup()
    _L0_attn_in = {k: v for k, v in _L0_attn_all.items() if k in ('bv_q', 'bv_k', 'bv_v')}
    del _L0_attn_all

    def _L0_cond2_setup():
        import jax, jax.numpy as jnp
        import numpy as np
        from jax import lax
        N, C_IN, L = (32, 64, 1024)
        C_OUT, K, GROUPS = (64, 9, 4)
        C_DIM, PAD, STRIDE = (128, 4, 1)
        key = jax.random.key(seed)
        k1, k2, k3, k4, k5 = jax.random.split(key, 5)
        x = jax.random.normal(k1, (N, C_IN, L), dtype=jnp.float32)
        c = jax.random.normal(k2, (N, C_DIM), dtype=jnp.float32)
        weight = jax.random.normal(k3, (C_OUT, C_IN // GROUPS, K), dtype=jnp.float32)
        c_weight = jax.random.normal(k4, (C_OUT, C_DIM), dtype=jnp.float32)
        bias = jax.random.normal(k5, (C_OUT,), dtype=jnp.float32)
        return {'x': x, 'c': c, 'weight': weight, 'c_weight': c_weight, 'bias': bias}
    _L0_cond2_all = _L0_cond2_setup()
    _L0_cond2_in = {k: v for k, v in _L0_cond2_all.items() if k in ('weight', 'c_weight')}
    del _L0_cond2_all

    def _L0_ffn_setup():
        import jax, jax.numpy as jnp
        import numpy as np
        IN_F = 1024
        OUT_F = 1024
        RANK = 8
        NUM_EXPERTS = 64
        TOP_K = 16
        ROUTER_DIM = 16
        ALPHA = 32
        SCALING = ALPHA / TOP_K
        BOTTLENECK = NUM_EXPERTS * RANK
        key = jax.random.key(seed)
        ks = jax.random.split(key, 5)
        x = jax.random.normal(ks[0], (4, 1024, IN_F), dtype=jnp.float32)
        bound_a = float(np.sqrt(6.0 / IN_F))
        A_w = jax.random.uniform(ks[1], (BOTTLENECK, IN_F), jnp.float32, -bound_a, bound_a)
        B_w = jax.random.normal(ks[2], (OUT_F, BOTTLENECK), dtype=jnp.float32) * 0.02
        Wq_w = jax.random.normal(ks[3], (ROUTER_DIM, IN_F), dtype=jnp.float32) * 0.02
        keys = jax.random.normal(ks[4], (NUM_EXPERTS, ROUTER_DIM), dtype=jnp.float32) * 0.01
        return {'x': x, 'A_w': A_w, 'B_w': B_w, 'Wq_w': Wq_w, 'keys': keys}
    _L0_ffn_all = _L0_ffn_setup()
    _L0_ffn_in = {k: v for k, v in _L0_ffn_all.items() if k in ('A_w', 'B_w', 'Wq_w', 'keys')}
    del _L0_ffn_all
    return {'x': x, 'cond_128': cond_128, 'fside_S_0': fside_S_0, 'L0_cond_W0': _L0_cond_in['W0'], 'L0_cond_b0': _L0_cond_in['b0'], 'L0_cond_W1': _L0_cond_in['W1'], 'L0_cond_b1': _L0_cond_in['b1'], 'L0_cond_W2': _L0_cond_in['W2'], 'L0_cond_b2': _L0_cond_in['b2'], 'L0_cond_weight': _L0_cond_in['weight'], 'L0_cond_bias_k': _L0_cond_in['bias_k'], 'L0_attn_bv_q': _L0_attn_in['bv_q'], 'L0_attn_bv_k': _L0_attn_in['bv_k'], 'L0_attn_bv_v': _L0_attn_in['bv_v'], 'L0_cond2_weight': _L0_cond2_in['weight'], 'L0_cond2_c_weight': _L0_cond2_in['c_weight'], 'L0_ffn_A_w': _L0_ffn_in['A_w'], 'L0_ffn_B_w': _L0_ffn_in['B_w'], 'L0_ffn_Wq_w': _L0_ffn_in['Wq_w'], 'L0_ffn_keys': _L0_ffn_in['keys']}

def reference(x, cond_128, fside_S_0, L0_cond_W0, L0_cond_b0, L0_cond_W1, L0_cond_b1, L0_cond_W2, L0_cond_b2, L0_cond_weight, L0_cond_bias_k, L0_attn_bv_q, L0_attn_bv_k, L0_attn_bv_v, L0_cond2_weight, L0_cond2_c_weight, L0_ffn_A_w, L0_ffn_B_w, L0_ffn_Wq_w, L0_ffn_keys):
    import jax
    import jax.numpy as jnp

    def _L0_cond_ref(x, embedding, W0, b0, W1, b1, W2, b2, weight, bias_k):
        import jax, jax.numpy as jnp
        import numpy as np
        K = 8
        T = 1.0
        D_EMBD = 128
        IN_C = 64
        OUT_C = 64
        BS = 32
        H = 1024
        HID = 128
        h = jax.nn.gelu(embedding @ W0 + b0, approximate=False)
        h = jax.nn.gelu(h @ W1 + b1, approximate=False)
        att = jax.nn.softmax((h @ W2 + b2) / T, axis=-1)
        agg_w = jnp.einsum('bk,koi->boi', att, weight[..., 0])
        agg_b = att @ bias_k
        out = jnp.einsum('boi,bih->boh', agg_w, x) + agg_b[:, :, None]
        return out

    def _L0_attn_ref(x, bv_q, bv_k, bv_v):
        import jax, jax.numpy as jnp
        import numpy as np
        HDC_DIM = 1024
        N_HEADS = 4
        HEAD_DIM = HDC_DIM // N_HEADS

        def _ste_sign(w):
            alpha = jnp.mean(jnp.abs(w), axis=-1, keepdims=True)
            hard = alpha * jnp.sign(w)
            hard = jnp.where(hard == 0, alpha, hard)
            return jax.lax.stop_gradient(hard - w) + w
        B, T, D = x.shape
        H, HD = (N_HEADS, HEAD_DIM)
        scale = HD ** (-0.5)
        q_bind = _ste_sign(bv_q)
        k_bind = _ste_sign(bv_k)
        v_bind = _ste_sign(bv_v)
        xh = x.reshape(B, T, H, HD)
        Q = xh * q_bind
        K = xh * k_bind
        V = xh * v_bind
        scores = jnp.einsum('bthd,bshd->bhts', Q, K) * scale
        causal = jnp.tril(jnp.ones((T, T), dtype=bool))
        attn = jnp.where(causal, jax.nn.sigmoid(scores * 4.0), 0.0)
        out = jnp.einsum('bhts,bshd->bthd', attn, V)
        return out.reshape(B, T, D)

    def _L0_cond2_ref(x, c, weight, c_weight, bias):
        import jax, jax.numpy as jnp
        import numpy as np
        from jax import lax
        N, C_IN, L = (32, 64, 1024)
        C_OUT, K, GROUPS = (64, 9, 4)
        C_DIM, PAD, STRIDE = (128, 4, 1)
        out = lax.conv_general_dilated(x, weight, window_strides=(STRIDE,), padding=[(PAD, PAD)], dimension_numbers=('NCH', 'OIH', 'NCH'), feature_group_count=GROUPS)
        ctx = jnp.einsum('nd,od->no', c, c_weight)
        out = out + ctx[:, :, None] + bias[None, :, None]
        return out

    def _L0_ffn_ref(x, A_w, B_w, Wq_w, keys):
        import jax, jax.numpy as jnp
        import numpy as np
        IN_F = 1024
        OUT_F = 1024
        RANK = 8
        NUM_EXPERTS = 64
        TOP_K = 16
        ROUTER_DIM = 16
        ALPHA = 32
        SCALING = ALPHA / TOP_K
        BOTTLENECK = NUM_EXPERTS * RANK
        q = jnp.einsum('bsd,rd->bsr', x, Wq_w)
        scores = jnp.einsum('bsr,er->bse', q, keys)
        top_vals, top_idx = jax.lax.top_k(scores, TOP_K)
        top_w = jax.nn.softmax(top_vals, axis=-1)
        gate = jnp.sum(jax.nn.one_hot(top_idx, NUM_EXPERTS, dtype=top_w.dtype) * top_w[..., None], axis=-2)
        z = jnp.einsum('bsd,nd->bsn', x, A_w)
        z = z.reshape(*z.shape[:-1], NUM_EXPERTS, RANK)
        z_gated = (z * gate[..., None]).reshape(*z.shape[:-2], BOTTLENECK)
        out = jnp.einsum('bsn,on->bso', z_gated, B_w) * SCALING
        return out
    x = x + _L0_attn_ref(_L0_cond_ref(x, cond_128, L0_cond_W0, L0_cond_b0, L0_cond_W1, L0_cond_b1, L0_cond_W2, L0_cond_b2, L0_cond_weight, L0_cond_bias_k), L0_attn_bv_q, L0_attn_bv_k, L0_attn_bv_v)
    x = x + _L0_ffn_ref(_L0_cond2_ref(x, cond_128, L0_cond2_weight, L0_cond2_c_weight, fside_S_0), L0_ffn_A_w, L0_ffn_B_w, L0_ffn_Wq_w, L0_ffn_keys)
    return x

_drawn_inputs = setup_inputs


def setup_inputs(seed=0):
    import zlib

    import numpy as np

    out = dict(_drawn_inputs(seed))
    spreads = {'L0_cond_b0': (0.0, 1.752), 'L0_cond_b1': (0.0, 0.61), 'L0_cond_b2': (0.0, 0.554)}
    factors = {'L0_attn_bv_q': 64.0, 'L0_attn_bv_k': 64.0}
    for name, (base, spread) in spreads.items():
        noise = np.random.default_rng([zlib.crc32(name.encode()), seed]).standard_normal(out[name].shape)
        drawn = base * np.exp(spread * noise) if base else spread * noise
        out[name] = jnp.asarray(drawn.astype(out[name].dtype))
    for name, factor in factors.items():
        out[name] = (out[name] * factor).astype(out[name].dtype)
    return out
```

```python
from contextlib import ExitStack

import concourse.bass as bass
from concourse import mybir

F32 = mybir.dt.float32
F32R = mybir.dt.float32r
ALU = mybir.AluOpType
ACT = mybir.ActivationFunctionType
AX = mybir.AxisListType

B, S, D = 32, 64, 1024
P = 128
PAIRS = B // 2
H, HD = 4, 256
Q = 8
M = D // Q
HM = HD // Q
NK = 8
G, GC = 4, 16
TAPS, PAD = 9, 4
E, RANK, TOPK = 64, 8, 16
NB = E * RANK
RD = 16
NT = NB // P
ZW = (NB + E) // 2
XW = 132
SCALING = 2.0
LOWEST = -3.0e38
CH = 4
CW = S * S // CH


def adaln_attn_ffn_kernel(nc, x, emb_t, w0, b0, w1, b1, w2, b2, wk_n, wk_t, bias_k, bq, bk, bv,
                          toep, cw_t, fside, a_t, wq, keys_t, b_t, out):
    ctx = ExitStack()
    with ctx:
        def sb(name, shape, dt=F32):
            return ctx.enter_context(nc.sbuf_tensor(name, shape, dt))

        def ps(name, shape):
            return ctx.enter_context(nc.psum_tensor(name, shape, F32))

        def sem(name):
            return ctx.enter_context(nc.semaphore(name))

        agg_n = nc.dram_tensor("agg_n", (B, S * S), F32, kind="Internal").ap()
        agg_t = nc.dram_tensor("agg_t", (B, S * S), F32, kind="Internal").ap()
        bias_d = nc.dram_tensor("bias_d", (B, 2 * S), F32, kind="Internal").ap()

        ident = sb("ident", [P, P])
        ones = sb("ones", [P, P])
        chunk_mask = sb("chunk_mask", [CH * NK, CH])
        mask_st = sb("mask_st", [P, S])
        mask_ts = sb("mask_ts", [P, S])
        a_raw = sb("a_raw", [P, Q, NB])
        b_raw = sb("b_raw", [P, NT, D])
        a_hi = sb("a_hi", [P, Q, NB + E], F32R)
        a_lo = sb("a_lo", [P, Q, NB + E], F32R)
        b_hi = sb("b_hi", [P, NT, D], F32R)
        b_lo = sb("b_lo", [P, NT, D], F32R)
        toep_sb = sb("toep_sb", [P, G, 2, P])
        vb = sb("vb", [P, H, HD])
        qk = sb("qk", [P, 2 * H])
        emb_sb = sb("emb_sb", [P, B])
        w0_sb = sb("w0_sb", [P, P])
        w1_sb = sb("w1_sb", [P, P])
        w2_sb = sb("w2_sb", [P, NK])
        b01 = sb("b01", [P, 2])
        b2_sb = sb("b2_sb", [B, NK])
        wk_sb = sb("wk_sb", [CH * NK, 2, CW])
        bias_k_sb = sb("bias_k_sb", [NK, S])
        bqk = sb("bqk", [P, 2, 2 * H])
        cw_sb = sb("cw_sb", [P, S])
        fside_sb = sb("fside_sb", [B, S])
        wq_sb = sb("wq_sb", [RD, Q, M])
        keys_sb = sb("keys_sb", [RD, E])
        h0 = sb("h0", [P, B])
        h1 = sb("h1", [P, B])
        lg = sb("lg", [B, 4, NK])
        lgs = sb("lgs", [B, 4])
        att_rep = sb("att_rep", [B, CH, NK])
        att4 = sb("att4", [CH * NK, CH, B])
        bias_sb = sb("bias_sb", [B, 2, S])
        bqk_t = sb("bqk_t", [P, 4, 2, 2 * H])
        bqk_a = sb("bqk_a", [P, 2, H])
        vraw = sb("vraw", [P, H, HD])
        valpha = sb("valpha", [P, 2, H])
        x_sb = [sb(f"x_sb{i}", [P, H, HD]) for i in range(2)]
        x1_sb = [sb(f"x1_sb{i}", [P, Q, XW]) for i in range(2)]
        wt_sb = [sb(f"wt_sb{i}", [P, P]) for i in range(2)]
        wn_sb = [sb(f"wn_sb{i}", [P, P]) for i in range(2)]
        bias_bc = [sb(f"bias_bc{i}", [P, 2, 2, S]) for i in range(2)]
        yT = sb("yT", [P, 2 * H, P])
        kT = sb("kT", [P, 2 * H, P])
        th = sb("th", [P, H, S])
        attnT = sb("attnT", [P, H, S])
        bm = sb("bm", [P, S])
        cprod = sb("cprod", [P, H, S])
        cvec = sb("cvec", [P, H])
        mblk = sb("mblk", [P, H, P])
        r_sb = sb("r_sb", [P, H, HD])
        xg = sb("xg", [P, 2, G, XW])
        c_sb = sb("c_sb", [P, Q, P])
        c_hi = sb("c_hi", [P, Q, P], F32R)
        c_lo = sb("c_lo", [P, Q, P], F32R)
        rs = sb("rs", [P, 6, E])
        gate = sb("gate", [P, 2, E])
        top8 = sb("top8", [P, 2, 8])
        gsum = sb("gsum", [P, 2])
        zg = sb("zg", [P, NB])
        zt_hi = sb("zt_hi", [P, NT, P], F32R)
        zt_lo = sb("zt_lo", [P, NT, P], F32R)
        o_sb = sb("o_sb", [P, 2, D // 2])

        ps_y = [ps(f"ps_y{i}", [P, 512]) for i in range(2)]
        ps_c = [ps(f"ps_c{i}", [P, 512]) for i in range(2)]
        ps_z = [ps(f"ps_z{i}", [P, 512]) for i in range(2)]
        ps_s = ps("ps_s", [P, 512])
        ps_t = ps("ps_t", [P, 512])

        small_in = sem("small_in")
        small_in2 = sem("small_in2")
        bv_in = sem("bv_in")
        toep_in = sem("toep_in")
        a_in = sem("a_in")
        b_in = sem("b_in")
        const_step = sem("const_step")
        consts = sem("consts")
        cond_mm = sem("cond_mm")
        cond_act = sem("cond_act")
        cond_dve = sem("cond_dve")
        bind_dve = sem("bind_dve")
        bind_mm = sem("bind_mm")
        qk_abs = sem("qk_abs")
        v_abs = sem("v_abs")
        v_alpha = sem("v_alpha")
        v_step = sem("v_step")
        scratch_out = sem("scratch_out")
        wqk_mm = sem("wqk_mm")
        split_hi = sem("split_hi")
        split_lo = sem("split_lo")
        split_lo_b = sem("split_lo_b")
        x_in = [sem(f"x_in{i}") for i in range(2)]
        par_in = [sem(f"par_in{i}") for i in range(2)]
        y_mm = sem("y_mm")
        y_rdy = sem("y_rdy")
        k_rdy = sem("k_rdy")
        s_mm = sem("s_mm")
        th_rdy = sem("th_rdy")
        attn_rdy = sem("attn_rdy")
        c_step = sem("c_step")
        m_mm = sem("m_mm")
        m_rdy = sem("m_rdy")
        ax_mm = sem("ax_mm")
        r_rdy = sem("r_rdy")
        x1_rdy = sem("x1_rdy")
        xg_in = sem("xg_in")
        c_mm = sem("c_mm")
        c_rdy = sem("c_rdy")
        chi_rdy = sem("chi_rdy")
        clo_rdy = sem("clo_rdy")
        z_mm = sem("z_mm")
        route = sem("route")
        bm_rdy = sem("bm_rdy")
        exp_rdy = sem("exp_rdy")
        gate_rdy = sem("gate_rdy")
        zg_rdy = sem("zg_rdy")
        t_mm = sem("t_mm")
        zhi_rdy = sem("zhi_rdy")
        zlo_rdy = sem("zlo_rdy")
        o_mm = sem("o_mm")
        o_rdy = sem("o_rdy")
        o_out = [sem(f"o_out{i}") for i in range(2)]
        ROUTE = 9
        XG16 = 2 * G * 16
        PAR16 = 5 * 16

        def wait(eng, s, value):
            if not (isinstance(value, int) and value <= 0):
                eng.wait_ge(s, value)

        def number(pair):
            return pair[0] * 2 + pair[1]

        def is_first(pair):
            return pair is not None and isinstance(pair[0], int) and number(pair) == 0

        def run(eng, step):
            step((0, 0), None, None)
            step((0, 1), (0, 0), None)
            step((1, 0), (0, 1), (0, 0))
            step((1, 1), (1, 0), (0, 1))
            with eng.Fori(1, PAIRS // 2 - 1) as i:
                step((i + 1, 0), (i, 1), (i, 0))
                step((i + 1, 1), (i + 1, 0), (i, 1))
            last = PAIRS // 2 - 1
            step(None, (last, 1), (last, 0))
            step(None, None, (last, 1))

        block = ctx.enter_context(nc.Block())

        @block.sync
        def _(sp):
            def load_pair(pair):
                n, par = number(pair), pair[1]
                wait(sp, x1_rdy, n * 2 - 2)
                sp.dma_start(x_sb[par][:].rearrange("p h d -> p (h d)"),
                             x[bass.ds(n * P, P), :]).then_inc(x_in[par], 16)

            def load_params(pair):
                n, par = number(pair), pair[1]
                wait(sp, c_rdy, n * 2 - 2)
                for j in range(2):
                    lo, hi = j * S, (j + 1) * S
                    for dst, src in ((wt_sb, agg_t), (wn_sb, agg_n)):
                        sp.dma_start(dst[par][lo:hi, lo:hi],
                                     src[bass.ds(n * 2 + j, 1), :].rearrange("a (r c) -> (a r) c", c=S)
                                     ).then_inc(par_in[par], 16)
                sp.dma_start(bias_bc[par][:].rearrange("p b k s -> p (b k s)"),
                             bias_d[bass.ds(n * 2, 2), :].rearrange("(a b) s -> a (b s)", a=1)
                             .to_broadcast([P, 4 * S])).then_inc(par_in[par], 16)

            def regroup(pair):
                n, par = number(pair), pair[1]
                wait(sp, x1_rdy, n * 2 + 2)
                wait(sp, c_mm, n * 2)
                for j in range(2):
                    for g in range(G):
                        lo = j * S + g * GC
                        sp.dma_start(xg[:, j, g, 0:M + 1],
                                     x1_sb[par][lo:lo + GC, :, 0:M + 1]).then_inc(xg_in, 16)

            def store(pair, j):
                n = number(pair)
                wait(sp, o_rdy, n * 2 + 1 + j)
                sp.dma_start(out[bass.ds(n * P, P), j * 512:(j + 1) * 512],
                             o_sb[:, j, :]).then_inc(o_out[j], 16)

            sp.dma_start(emb_sb[:], emb_t).then_inc(small_in, 16)
            sp.dma_start(w0_sb[:], w0).then_inc(small_in, 16)
            sp.dma_start(w1_sb[:], w1).then_inc(small_in, 16)
            sp.dma_start(w2_sb[:], w2).then_inc(small_in, 16)
            load_pair((0, 0))
            sp.dma_start(vraw[:].rearrange("p h d -> p (h d)"), bv.to_broadcast([P, D])).then_inc(bv_in, 16)
            load_pair((0, 1))
            sp.dma_start(toep_sb[:], toep).then_inc(toep_in, 16)
            sp.dma_start(a_raw[:], a_t).then_inc(a_in, 16)
            sp.dma_start(b_raw[:], b_t).then_inc(b_in, 16)
            sp.wait_ge(scratch_out, (2 * CH + 1) * 16)
            sp.wait_ge(consts, 1)
            load_params((0, 0))
            load_params((0, 1))

            def step(a, c, f):
                if f is not None and not is_first(f):
                    store((f[0], 0) if f[1] else (f[0] - 1, 1), 1)
                if c is not None:
                    regroup(c)
                nxt = after(a)
                if nxt is not None and not (isinstance(nxt[0], int) and number(nxt) < 2):
                    load_pair(nxt)
                    load_params(nxt)
                if f is not None:
                    store(f, 0)

            def after(a):
                if a is None:
                    return None
                return (a[0], 1) if a[1] == 0 else (a[0] + 1, 0)

            step((0, 0), None, None)
            step((0, 1), (0, 0), None)
            step((1, 0), (0, 1), (0, 0))
            step((1, 1), (1, 0), (0, 1))
            with sp.Fori(1, PAIRS // 2 - 2) as i:
                step((i + 1, 0), (i, 1), (i, 0))
                step((i + 1, 1), (i + 1, 0), (i, 1))
            last = PAIRS // 2 - 1
            step((last, 0), (last - 1, 1), (last - 1, 0))
            step(None, (last, 0), (last - 1, 1))
            step(None, (last, 1), (last, 0))
            step(None, None, (last, 1))
            store((last, 1), 1)
            sp.wait_ge(o_out[0], PAIRS * 16)
            sp.wait_ge(o_out[1], PAIRS * 16)

        @block.gpsimd
        def _(pool):
            nc.gpsimd.memset(ident[:], 0.0).then_inc(const_step, 1)
            nc.gpsimd.memset(chunk_mask[:], 1.0).then_inc(const_step, 1)
            nc.gpsimd.memset(mask_st[:], 0.5).then_inc(const_step, 1)
            nc.gpsimd.memset(mask_ts[:], 0.5).then_inc(const_step, 1)
            nc.gpsimd.memset(ones[:], 1.0)
            pool.wait_ge(const_step, 4)
            nc.gpsimd.affine_select(out=ident[:], in_=ident[:], compare_op=ALU.not_equal, fill=1.0,
                                    base=0, pattern=[[-1, P]], channel_multiplier=1)
            nc.gpsimd.affine_select(out=chunk_mask[:], in_=chunk_mask[:], compare_op=ALU.is_ge, fill=0.0,
                                    base=0, pattern=[[-NK, CH]], channel_multiplier=1).then_inc(const_step, 1)
            pool.wait_ge(const_step, 5)
            nc.gpsimd.affine_select(out=chunk_mask[:], in_=chunk_mask[:], compare_op=ALU.is_ge, fill=0.0,
                                    base=NK - 1, pattern=[[NK, CH]], channel_multiplier=-1
                                    ).then_inc(const_step, 1)
            for j, lo in enumerate((0, S)):
                rows = slice(lo, lo + S)
                pool.wait_ge(const_step, 6 + 2 * j)
                nc.gpsimd.affine_select(out=mask_st[rows], in_=mask_st[rows], compare_op=ALU.is_ge, fill=0.0,
                                        base=0, pattern=[[1, S]], channel_multiplier=-1
                                        ).then_inc(const_step, 1)
                pool.wait_ge(const_step, 7 + 2 * j)
                last = nc.gpsimd.affine_select(out=mask_ts[rows], in_=mask_ts[rows], compare_op=ALU.is_ge,
                                               fill=0.0, base=0, pattern=[[-1, S]], channel_multiplier=1
                                               ).then_inc(const_step, 1)
            pool.wait_ge(const_step, 10)
            for i in range(2):
                nc.gpsimd.memset(wt_sb[i][:], 0.0)
                last = nc.gpsimd.memset(wn_sb[i][:], 0.0)
            last.then_inc(consts, 1)
            for i in range(2):
                nc.gpsimd.memset(x1_sb[i][:], 0.0)
            nc.gpsimd.memset(mblk[:], 0.0).then_inc(consts, 1)
            pool.wait_ge(bv_in, 16)
            nc.gpsimd.tensor_scalar(vb[:], vraw[:], 0.0, 2.0, ALU.is_ge, ALU.mult).then_inc(v_step, 1)
            pool.wait_ge(v_step, 1)
            nc.gpsimd.tensor_scalar(vb[:], vb[:], -1.0, None, ALU.add).then_inc(v_step, 1)
            pool.wait_ge(v_step, 2)
            pool.wait_ge(v_alpha, 2)
            nc.gpsimd.tensor_tensor(vb[:], vb[:], valpha[:, 1, :].unsqueeze(2).to_broadcast([P, H, HD]),
                                    ALU.mult).then_inc(v_step, 1)
            pool.wait_ge(v_step, 3)
            nc.gpsimd.tensor_tensor(vb[:], vb[:], vraw[:], ALU.subtract).then_inc(v_step, 1)
            pool.wait_ge(v_step, 4)
            nc.gpsimd.tensor_tensor(vb[:], vb[:], vraw[:], ALU.add).then_inc(v_step, 1)

            def residual(pair):
                n, par = number(pair), pair[1]
                wait(pool, r_rdy, n * 4 + 4)
                for j in range(2):
                    wait(pool, o_rdy, n * 2 - 3 + j)
                    ph = slice(4 * j, 4 * j + 4)
                    by_phase = lambda t: t[:].rearrange("p h (q m) -> p q h m", q=Q)[:, ph]
                    nc.gpsimd.tensor_tensor(
                        x1_sb[par][:, ph, j:j + M].rearrange("p q (h m) -> p q h m", h=H),
                        by_phase(r_sb), by_phase(x_sb[par]), ALU.add).then_inc(x1_rdy, 1)

            def bind_k(pair):
                n = number(pair)
                wait(pool, y_rdy, n * 2 + 2)
                wait(pool, s_mm, n)
                nc.gpsimd.tensor_tensor(kT[:], yT[:], qk[:].unsqueeze(2).to_broadcast([P, 2 * H, P]),
                                        ALU.mult).then_inc(k_rdy, 1)

            def conv_low(pair):
                n = number(pair)
                wait(pool, chi_rdy, n + 1)
                nc.gpsimd.tensor_tensor(c_lo[:], c_sb[:], c_hi[:].bitcast(F32),
                                        ALU.subtract).then_inc(clo_rdy, 1)

            pool.wait_ge(bind_dve, 7)
            def step(a, c, f):
                if c is not None:
                    residual(c)
                if a is not None:
                    bind_k(a)
                if is_first(a):
                    pool.wait_ge(split_hi, 2)
                    nc.gpsimd.tensor_tensor(b_lo[:], b_raw[:], b_hi[:].bitcast(F32),
                                            ALU.subtract).then_inc(split_lo_b, 1)
                if c is not None:
                    conv_low(c)

            run(pool, step)

        @block.scalar
        def _(act):
            act.dma_start(b01[:, 0:1], b0).then_inc(small_in2, 16)
            act.dma_start(b01[:, 1:2], b1).then_inc(small_in2, 16)
            act.dma_start(b2_sb[:], b2.to_broadcast([B, NK])).then_inc(small_in2, 16)
            act.dma_start(bqk[:, 0, :], bq).then_inc(small_in2, 16)
            act.dma_start(bqk[:, 1, :], bk).then_inc(small_in2, 16)
            act.dma_start(wk_sb[:, 0, :], wk_n).then_inc(small_in2, 16)
            act.dma_start(wk_sb[:, 1, :], wk_t).then_inc(small_in2, 16)
            act.dma_start(bias_k_sb[:], bias_k).then_inc(small_in2, 16)
            act.dma_start(cw_sb[:], cw_t).then_inc(small_in2, 16)
            act.dma_start(fside_sb[:], fside.to_broadcast([B, S])).then_inc(small_in2, 16)
            act.dma_start(wq_sb[:].rearrange("r q m -> r (q m)"), wq).then_inc(small_in2, 16)
            act.dma_start(keys_sb[:], keys_t).then_inc(small_in2, 16)
            act.wait_ge(small_in2, 12 * 16)
            nc.scalar.activation(bqk_t[:, 0], bqk[:], ACT.Abs).then_inc(qk_abs, 1)
            act.wait_ge(cond_mm, 1)
            nc.scalar.activation(h0[:], ps_y[0][:, 0:B], ACT.Gelu, bias=b01[:, 0:1]).then_inc(cond_act, 1)
            act.wait_ge(cond_mm, 2)
            nc.scalar.activation(h1[:], ps_y[1][:, 0:B], ACT.Gelu, bias=b01[:, 1:2]).then_inc(cond_act, 1)
            act.wait_ge(cond_dve, 3)
            nc.scalar.activation(lg[:, 2, :], lg[:, 1, :], ACT.Exp, accum_out=lgs[:, 1:2]).then_inc(cond_act, 1)
            for j in range(2):
                act.wait_ge(cond_mm, 7 + j)
                nc.scalar.activation(r_sb[:].rearrange("p h d -> p (h d)")[:, j * 512:(j + 1) * 512],
                                     ps_z[j][:], ACT.Copy).then_inc(cond_act, 1)
            act.wait_ge(cond_act, 5)
            for c in range(CH):
                act.dma_start(agg_t[:, c * CW:(c + 1) * CW],
                              r_sb[c * B:(c + 1) * B].rearrange("p h d -> p (h d)")).then_inc(scratch_out, 16)
            act.wait_ge(cond_dve, 11)
            for c in range(CH):
                act.dma_start(agg_n[:, c * CW:(c + 1) * CW],
                              kT[c * B:(c + 1) * B].rearrange("p q m -> p (q m)")).then_inc(scratch_out, 16)
            act.dma_start(bias_d, bias_sb[:].rearrange("b k s -> b (k s)")).then_inc(scratch_out, 16)
            act.wait_ge(bv_in, 16)
            nc.scalar.activation(yT[:].rearrange("p q m -> p (q m)"), vraw[:].rearrange("p h d -> p (h d)"),
                                 ACT.Abs).then_inc(v_abs, 1)

            def split_weights():
                act.wait_ge(a_in, 16)
                nc.scalar.activation(a_hi[:, :, 0:NB], a_raw[:], ACT.Copy).then_inc(split_hi, 1)
                act.wait_ge(b_in, 16)
                nc.scalar.activation(b_hi[:], b_raw[:], ACT.Copy).then_inc(split_hi, 1)
                act.wait_ge(wqk_mm, 1)
                nc.scalar.activation(a_hi[:, :, NB:NB + E], ps_z[1][:].rearrange("p (q e) -> p q e", q=Q),
                                     ACT.Copy).then_inc(split_hi, 1)

            def router_exp(pair):
                n = number(pair)
                wait(act, route, n * ROUTE + 2)
                nc.scalar.activation(rs[:, 4, :], rs[:, 3, :], ACT.Exp).then_inc(exp_rdy, 1)

            def scores_tanh(pair):
                n = number(pair)
                wait(act, s_mm, n + 1)
                wait(act, c_step, n * 2)
                for j in range(2):
                    rows = slice(j * S, (j + 1) * S)
                    nc.scalar.activation(th[rows], ps_s[rows].rearrange("p (h t) -> p h t", h=H)[:, :, rows],
                                         ACT.Tanh, scale=2.0 * HD ** -0.5).then_inc(th_rdy, 1)

            def m_out(pair):
                n = number(pair)
                wait(act, m_mm, n + 1)
                wait(act, ax_mm, n * 2)
                for j in range(2):
                    rows = slice(j * S, (j + 1) * S)
                    nc.scalar.activation(mblk[rows, :, rows], ps_s[rows, 0:H * S]
                                         .rearrange("p (h t) -> p h t", h=H), ACT.Copy).then_inc(m_rdy, 1)

            def zt_high(pair):
                n = number(pair)
                wait(act, t_mm, n + 1)
                wait(act, o_mm, n * 2)
                nc.scalar.activation(zt_hi[:].rearrange("p a b -> p (a b)"), ps_t[:],
                                     ACT.Copy).then_inc(zhi_rdy, 1)

            def conv_high(pair):
                n = number(pair)
                wait(act, c_rdy, n * 2 + 2)
                wait(act, z_mm, n)
                nc.scalar.activation(c_hi[:], c_sb[:], ACT.Copy).then_inc(chi_rdy, 1)

            def step(a, c, f):
                if f is not None:
                    router_exp(f)
                if a is not None:
                    scores_tanh(a)
                    m_out(a)
                if is_first(a):
                    split_weights()
                if f is not None:
                    zt_high(f)
                if c is not None:
                    conv_high(c)

            run(act, step)

        @block.vector
        def _(dve):
            dve.wait_ge(small_in2, 12 * 16)
            dve.wait_ge(cond_mm, 3)
            nc.vector.tensor_tensor(lg[:, 0, :], ps_c[0][0:B, 0:NK], b2_sb[:], ALU.add).then_inc(cond_dve, 1)
            dve.wait_ge(cond_dve, 1)
            nc.vector.reduce_max(lgs[:, 0:1], lg[:, 0, :], AX.X).then_inc(cond_dve, 1)
            dve.wait_ge(cond_dve, 2)
            nc.vector.tensor_scalar(lg[:, 1, :], lg[:, 0, :], lgs[:, 0:1], None, ALU.subtract).then_inc(cond_dve, 1)
            dve.wait_ge(cond_act, 3)
            nc.vector.reciprocal(lgs[:, 2:3], lgs[:, 1:2]).then_inc(cond_dve, 1)
            dve.wait_ge(cond_dve, 4)
            nc.vector.tensor_scalar(att_rep[:], lg[:, 2:3, :].to_broadcast([B, CH, NK]),
                                    lgs[:, 2:3], None, ALU.mult).then_inc(cond_dve, 1)
            dve.wait_ge(cond_mm, 4)
            dve.wait_ge(const_step, 10)
            nc.vector.tensor_tensor(att4[:], ps_c[1][0:CH * NK, 0:B].unsqueeze(1).to_broadcast([CH * NK, CH, B]),
                                    chunk_mask[:].unsqueeze(2).to_broadcast([CH * NK, CH, B]),
                                    ALU.mult).then_inc(cond_dve, 1)
            for j in range(2):
                dve.wait_ge(cond_mm, 5 + j)
                nc.vector.tensor_copy(kT[:].rearrange("p q m -> p (q m)")[:, j * 512:(j + 1) * 512],
                                      ps_y[j][:]).then_inc(cond_dve, 1)
            dve.wait_ge(cond_mm, 10)
            nc.vector.tensor_copy(bias_sb[:, 0, :], ps_s[0:B, 0:S]).then_inc(cond_dve, 1)
            nc.vector.tensor_tensor(bias_sb[:, 1, :], ps_s[0:B, S:2 * S], fside_sb[:], ALU.add).then_inc(cond_dve, 1)
            dve.wait_ge(bind_mm, 1)
            nc.vector.reduce_sum(bqk_a[:], ps_t[:, 0:4 * H].rearrange("p (a h j) -> p a h j", a=2, j=2),
                                 AX.X).then_inc(cond_dve, 1)
            nc.vector.tensor_scalar(bqk_t[:, 1], bqk[:], 0.0, 2.0, ALU.is_ge, ALU.mult).then_inc(bind_dve, 1)
            dve.wait_ge(cond_dve, 11)
            nc.vector.tensor_scalar(bqk_a[:], bqk_a[:], 1.0 / HD, None, ALU.mult).then_inc(bind_dve, 1)
            dve.wait_ge(bind_dve, 2)
            nc.vector.tensor_scalar(bqk_t[:, 1], bqk_t[:, 1], -1.0, None, ALU.add).then_inc(bind_dve, 1)
            dve.wait_ge(bind_dve, 3)
            nc.vector.tensor_tensor(bqk_t[:, 2].rearrange("p a (h j) -> p a h j", j=2),
                                    bqk_t[:, 1].rearrange("p a (h j) -> p a h j", j=2),
                                    bqk_a[:].unsqueeze(3).to_broadcast([P, 2, H, 2]), ALU.mult).then_inc(bind_dve, 1)
            dve.wait_ge(bind_dve, 4)
            nc.vector.tensor_tensor(bqk_t[:, 2], bqk_t[:, 2], bqk[:], ALU.subtract).then_inc(bind_dve, 1)
            dve.wait_ge(bind_dve, 5)
            nc.vector.tensor_tensor(bqk_t[:, 3], bqk_t[:, 2], bqk[:], ALU.add).then_inc(bind_dve, 1)
            dve.wait_ge(bind_dve, 6)
            nc.vector.tensor_tensor(qk[:], bqk_t[:, 3, 0, :], bqk_t[:, 3, 1, :], ALU.mult).then_inc(bind_dve, 1)
            dve.wait_ge(v_abs, 1)
            nc.vector.tensor_reduce(valpha[:, 0, :],
                                    yT[:].rearrange("p (h j) c -> p h (j c)", h=H), AX.X, ALU.add).then_inc(v_alpha, 1)
            dve.wait_ge(v_alpha, 1)
            nc.vector.tensor_scalar(valpha[:, 1, :], valpha[:, 0, :], 1.0 / HD, None, ALU.mult).then_inc(v_alpha, 1)
            dve.wait_ge(scratch_out, (2 * CH + 1) * 16)

            def y_out(pair):
                n, par = number(pair), pair[1]
                wait(dve, s_mm, n)
                bias = bias_bc[par][:, :, 0, :].unsqueeze(1).to_broadcast([P, 4, 2, S])
                for j in range(2):
                    wait(dve, y_mm, n * 2 + 1 + j)
                    nc.vector.tensor_tensor(yT[:, 4 * j:4 * j + 4].rearrange("p a (b t) -> p a b t", b=2),
                                            ps_y[j][:].rearrange("p (a b t) -> p a b t", a=4, b=2),
                                            bias, ALU.add).then_inc(y_rdy, 1)

            def bias_mask(pair, j):
                par = pair[1]
                rows = slice(j * S, (j + 1) * S)
                nc.vector.tensor_tensor(bm[rows], mask_ts[rows], bias_bc[par][rows, j, 0, :],
                                        ALU.mult).then_inc(bm_rdy, 1)

            def router(a, f):
                n = number(f)
                at = lambda k: n * ROUTE + k
                scores = ps_z[1][:, ZW - E:ZW]
                wait(dve, z_mm, n + 1)
                nc.vector.tensor_copy(rs[:, 0, :], scores)
                nc.vector.max(top8[:, 0, :], scores).then_inc(route, 1)
                wait(dve, route, at(1))
                nc.vector.tensor_scalar(rs[:, 3, :], scores, top8[:, 0, 0:1], None,
                                        ALU.subtract).then_inc(route, 1)
                nc.vector.match_replace(rs[:, 1, :], top8[:, 0, :], scores, LOWEST).then_inc(route, 1)
                wait(dve, route, at(3))
                if a is not None:
                    bias_mask(a, 0)
                else:
                    nc.vector.tensor_copy(gate[:, 0, 0:1], top8[:, 0, 0:1])
                nc.vector.max(top8[:, 1, :], rs[:, 1, :]).then_inc(route, 1)
                wait(dve, route, at(4))
                if a is not None:
                    bias_mask(a, 1)
                else:
                    nc.vector.tensor_copy(gate[:, 0, 0:1], top8[:, 0, 0:1])
                nc.vector.match_replace(rs[:, 2, :], top8[:, 1, :], rs[:, 1, :], LOWEST).then_inc(route, 1)
                wait(dve, route, at(5))
                nc.vector.tensor_tensor(rs[:, 5, :], rs[:, 2, :], rs[:, 0, :], ALU.not_equal).then_inc(route, 1)
                wait(dve, exp_rdy, n + 1)
                wait(dve, route, at(6))
                nc.vector.tensor_tensor(gate[:, 0, :], rs[:, 4, :], rs[:, 5, :], ALU.mult).then_inc(route, 1)
                wait(dve, route, at(7))
                nc.vector.reduce_sum(gsum[:, 0:1], gate[:, 0, :], AX.X).then_inc(route, 1)
                wait(dve, route, at(8))
                nc.vector.reciprocal(gsum[:, 1:2], gsum[:, 0:1]).then_inc(route, 1)
                wait(dve, route, at(9))
                nc.vector.tensor_scalar(gate[:, 1, :], gate[:, 0, :], gsum[:, 1:2], SCALING,
                                        ALU.mult, ALU.mult).then_inc(gate_rdy, 1)
                wait(dve, gate_rdy, n + 1)
                wait(dve, t_mm, n)
                e0 = ZW // RANK
                for lo, hi, bank in ((0, e0, 0), (e0, E, 1)):
                    nc.vector.tensor_tensor(
                        zg[:, lo * RANK:hi * RANK].rearrange("p (e r) -> p e r", r=RANK),
                        ps_z[bank][:, 0:(hi - lo) * RANK].rearrange("p (e r) -> p e r", r=RANK),
                        gate[:, 1, lo:hi].unsqueeze(2).to_broadcast([P, hi - lo, RANK]),
                        ALU.mult).then_inc(zg_rdy, 1)

            def masked(pair):
                n = number(pair)
                wait(dve, th_rdy, n * 2 + 2)
                wait(dve, m_mm, n)
                nc.vector.scalar_tensor_tensor(out=attnT[:], in0=th[:], scalar=1.0,
                                               in1=mask_st[:].unsqueeze(1).to_broadcast([P, H, S]),
                                               op0=ALU.add, op1=ALU.mult).then_inc(attn_rdy, 1)
                wait(dve, bm_rdy, n * 2 + 2)
                nc.vector.scalar_tensor_tensor(out=cprod[:], in0=th[:], scalar=1.0,
                                               in1=bm[:].unsqueeze(1).to_broadcast([P, H, S]),
                                               op0=ALU.add, op1=ALU.mult).then_inc(c_step, 1)
                wait(dve, c_step, n * 2 + 1)
                nc.vector.reduce_sum(cvec[:], cprod[:], AX.X).then_inc(c_step, 1)

            def conv_out(pair):
                n, par = number(pair), pair[1]
                wait(dve, chi_rdy, n)
                wait(dve, clo_rdy, n)
                for j in range(2):
                    wait(dve, c_mm, n * 2 + 1 + j)
                    bias = bias_bc[par][:, j, 1, :].rearrange("p (g o) -> p g o", g=G)
                    nc.vector.tensor_tensor(
                        c_sb[:, :, j * S:(j + 1) * S].rearrange("p r (g o) -> p r g o", g=G),
                        ps_c[j][:].rearrange("p (g r o) -> p r g o", g=G, r=Q),
                        bias.unsqueeze(1).to_broadcast([P, Q, G, GC]), ALU.add).then_inc(c_rdy, 1)

            def zt_low(pair):
                n = number(pair)
                wait(dve, zhi_rdy, n + 1)
                wait(dve, o_mm, n * 2)
                nc.vector.tensor_tensor(zt_lo[:].rearrange("p a b -> p (a b)"), ps_t[:],
                                        zt_hi[:].bitcast(F32).rearrange("p a b -> p (a b)"),
                                        ALU.subtract).then_inc(zlo_rdy, 1)

            def attn_out(pair):
                n = number(pair)
                wait(dve, c_step, n * 2 + 2)
                wait(dve, x1_rdy, n * 2)
                for h in range(H):
                    if h % 2 == 0:
                        wait(dve, ax_mm, n * 2 + 1 + h // 2)
                    nc.vector.scalar_tensor_tensor(
                        out=r_sb[:, h, :], in0=ps_y[h // 2][:, (h % 2) * HD:(h % 2 + 1) * HD],
                        scalar=cvec[:, h:h + 1], in1=vb[:, h, :], op0=ALU.add, op1=ALU.mult).then_inc(r_rdy, 1)

            def final(pair, j):
                n, par = number(pair), pair[1]
                wait(dve, o_mm, n * 2 + 1 + j)
                wait(dve, o_out[j], n * 16)
                nc.vector.tensor_tensor(o_sb[:, j, :].rearrange("p (q m) -> p q m", q=4),
                                        ps_z[j][:].rearrange("p (q m) -> p q m", q=4),
                                        x1_sb[par][:, 4 * j:4 * j + 4, j:j + M], ALU.add).then_inc(o_rdy, 1)

            def step(a, c, f):
                if f is not None and not is_first(f):
                    final((f[0], 0) if f[1] else (f[0] - 1, 1), 1)
                if a is not None:
                    y_out(a)
                if f is not None:
                    router(a, f)
                elif a is not None:
                    bias_mask(a, 0)
                    bias_mask(a, 1)
                if a is not None:
                    masked(a)
                if c is not None:
                    conv_out(c)
                if f is not None:
                    zt_low(f)
                if a is not None:
                    if is_first(a):
                        dve.wait_ge(v_step, 5)
                    attn_out(a)
                if is_first(a):
                    dve.wait_ge(split_hi, 3)
                    nc.vector.tensor_tensor(a_lo[:, :, 0:NB], a_raw[:], a_hi[:, :, 0:NB].bitcast(F32),
                                            ALU.subtract).then_inc(split_lo, 1)
                    nc.vector.tensor_tensor(a_lo[:, :, NB:NB + E],
                                            ps_z[1][:].rearrange("p (q e) -> p q e", q=Q),
                                            a_hi[:, :, NB:NB + E].bitcast(F32), ALU.subtract).then_inc(split_lo, 1)
                if f is not None:
                    final(f, 0)

            run(dve, step)
            final((PAIRS // 2 - 1, 1), 1)

        @block.tensor
        def _(pe):
            pe.wait_ge(small_in, 4 * 16)
            nc.tensor.matmul(ps_y[0][:, 0:B], w0_sb[:], emb_sb[:], start=True, stop=True).then_inc(cond_mm, 1)
            pe.wait_ge(cond_act, 1)
            nc.tensor.matmul(ps_y[1][:, 0:B], w1_sb[:], h0[:], start=True, stop=True).then_inc(cond_mm, 1)
            pe.wait_ge(const_step, 10)
            pe.wait_ge(qk_abs, 1)
            nc.tensor.matmul(ps_t[:, 0:4 * H], ones[:], bqk_t[:, 0].rearrange("p a t -> p (a t)"),
                             start=True, stop=True).then_inc(bind_mm, 1)
            pe.wait_ge(cond_act, 2)
            nc.tensor.matmul(ps_c[0][0:B, 0:NK], h1[:], w2_sb[:], start=True, stop=True).then_inc(cond_mm, 1)
            pe.wait_ge(cond_dve, 5)
            nc.tensor.matmul(ps_c[1][0:CH * NK, 0:B], att_rep[:].rearrange("b c k -> b (c k)"),
                             ident[0:B, 0:B], start=True, stop=True).then_inc(cond_mm, 1)
            pe.wait_ge(cond_dve, 6)
            for form, bank in ((0, ps_y), (1, ps_z)):
                for j in range(2):
                    nc.tensor.matmul(bank[j][:], att4[:].rearrange("r c b -> r (c b)"),
                                     wk_sb[:, form, j * 512:(j + 1) * 512], start=True, stop=True).then_inc(cond_mm, 1)
            nc.tensor.matmul(ps_s[0:B, 0:S], att4[0:NK, 0, :], bias_k_sb[:], start=True, stop=True).then_inc(cond_mm, 1)
            nc.tensor.matmul(ps_s[0:B, S:2 * S], emb_sb[:], cw_sb[:], start=True, stop=True).then_inc(cond_mm, 1)
            pe.wait_ge(cond_act, 5)
            for q in range(Q):
                last = nc.tensor.matmul(ps_z[1][:, q * E:(q + 1) * E], wq_sb[:, q, :], keys_sb[:],
                                        start=True, stop=True)
            last.then_inc(wqk_mm, 1)
            pe.wait_ge(cond_dve, 11)

            def y_product(pair):
                n, par = number(pair), pair[1]
                wait(pe, x_in[par], pair[0] * 16 + 16)
                wait(pe, par_in[par], pair[0] * PAR16 + PAR16)
                for j in range(2):
                    wait(pe, r_rdy, n * 4 - 2 + 2 * j)
                    for k in range(4):
                        h, half = 2 * j + k // 2, k % 2
                        last = nc.tensor.matmul(ps_y[j][:, k * P:(k + 1) * P],
                                                x_sb[par][:, h, half * P:(half + 1) * P],
                                                wt_sb[par][:], start=True, stop=True)
                    last.then_inc(y_mm, 1)

            def scores(pair):
                n = number(pair)
                wait(pe, m_rdy, n * 2)
                wait(pe, k_rdy, n + 1)
                for h in range(H):
                    for k in range(2):
                        last = nc.tensor.matmul(ps_s[:, h * P:(h + 1) * P], kT[:, 2 * h + k, :],
                                                yT[:, 2 * h + k, :], start=(k == 0), stop=(k == 1))
                last.then_inc(s_mm, 1)

            def m_product(pair):
                n, par = number(pair), pair[1]
                wait(pe, attn_rdy, n + 1)
                nc.tensor.matmul(ps_s[:, 0:H * S], wn_sb[par][:], attnT[:].rearrange("p h t -> p (h t)"),
                                 start=True, stop=True).then_inc(m_mm, 1)

            def attn_x(pair):
                n, par = number(pair), pair[1]
                wait(pe, m_rdy, n * 2 + 2)
                for h in range(H):
                    last = nc.tensor.matmul(ps_y[h // 2][:, (h % 2) * HD:(h % 2 + 1) * HD], mblk[:, h, :],
                                            x_sb[par][:, h, :], start=True, stop=True)
                    if h % 2:
                        last.then_inc(ax_mm, 1)

            def conv(pair):
                n = number(pair)
                wait(pe, xg_in, n * XG16 + XG16)
                for j in range(2):
                    wait(pe, c_rdy, n * 2 - 1 + j)
                    for g in range(G):
                        for k in range(2):
                            last = nc.tensor.matmul(ps_c[j][:, g * P:(g + 1) * P], xg[:, j, g, k:k + M],
                                                    toep_sb[:, g, k, :], start=(k == 0), stop=(k == 1))
                    last.then_inc(c_mm, 1)

            def z_product(pair):
                n = number(pair)
                wait(pe, clo_rdy, n + 1)
                wait(pe, o_rdy, n * 2)
                for q in range(Q):
                    for i, (w, m) in enumerate(((c_hi, a_hi), (c_hi, a_lo), (c_lo, a_hi))):
                        for j in range(2):
                            last = nc.tensor.matmul(ps_z[j][:, 0:ZW], w[:, q, :], m[:, q, j * ZW:(j + 1) * ZW],
                                                    start=(q == 0 and i == 0), stop=(q == Q - 1 and i == 2))
                last.then_inc(z_mm, 1)

            def turn(pair):
                n = number(pair)
                wait(pe, zg_rdy, n * 2 + 2)
                wait(pe, zlo_rdy, n)
                for k in range(NT):
                    last = nc.tensor.transpose(ps_t[:, k * P:(k + 1) * P], zg[:, k * P:(k + 1) * P], ident[:])
                last.then_inc(t_mm, 1)

            def out_product(pair, j):
                n = number(pair)
                if j == 0:
                    wait(pe, zlo_rdy, n + 1)
                cols = slice(j * 512, (j + 1) * 512)
                for k in range(NT):
                    for i, (w, m) in enumerate(((zt_hi, b_hi), (zt_hi, b_lo), (zt_lo, b_hi))):
                        last = nc.tensor.matmul(ps_z[j][:], w[:, k, :], m[:, k, cols],
                                                start=(k == 0 and i == 0), stop=(k == NT - 1 and i == 2))
                last.then_inc(o_mm, 1)

            def step(a, c, f):
                if a is not None:
                    y_product(a)
                if is_first(f):
                    pe.wait_ge(split_lo, 2)
                    pe.wait_ge(split_lo_b, 1)
                if f is not None:
                    z_product(f)
                if a is not None:
                    scores(a)
                if c is not None:
                    if is_first(c):
                        pe.wait_ge(toep_in, 16)
                    conv(c)
                if a is not None:
                    m_product(a)
                if f is not None:
                    turn(f)
                if a is not None:
                    if is_first(a):
                        pe.wait_ge(consts, 2)
                    attn_x(a)
                if f is not None:
                    out_product(f, 0)
                    out_product(f, 1)

            run(pe, step)


def kernel(**inputs):
    import numpy as np
    import concourse.bacc as bacc
    from concourse.bass_utils import run_bass_kernel_spmd

    inp = {k: np.asarray(v) for k, v in inputs.items()}
    x = inp["x"].reshape(B * S, H, HM, Q).transpose(0, 1, 3, 2).reshape(B * S, D)
    wk = inp["L0_cond_weight"][..., 0]

    def chunks(w):
        return w.reshape(NK, CH, CW).transpose(1, 0, 2).reshape(CH * NK, CW)

    def tile_columns(w):
        return w.reshape(H, HM, 2, 4).transpose(3, 1, 0, 2).reshape(P, 2 * H)

    w = inp["L0_cond2_weight"].reshape(G, GC, GC, TAPS)
    toep = np.zeros((GC, Q, G, 2, Q, GC), w.dtype)
    for q in range(Q):
        p = q + PAD if q < PAD else q - PAD
        for k in range(2):
            for r in range(Q):
                tap = p + Q * k - r
                if 0 <= tap < TAPS:
                    toep[:, q, :, k, r, :] = w[:, :, :, tap].transpose(2, 0, 1)
    arrays = {
        "x": x,
        "emb_t": inp["cond_128"].T,
        "w0": inp["L0_cond_W0"], "b0": inp["L0_cond_b0"].reshape(P, 1),
        "w1": inp["L0_cond_W1"], "b1": inp["L0_cond_b1"].reshape(P, 1),
        "w2": inp["L0_cond_W2"], "b2": inp["L0_cond_b2"].reshape(1, NK),
        "wk_n": chunks(wk.reshape(NK, S * S)),
        "wk_t": chunks(wk.transpose(0, 2, 1).reshape(NK, S * S)),
        "bias_k": inp["L0_cond_bias_k"],
        "bq": tile_columns(inp["L0_attn_bv_q"]),
        "bk": tile_columns(inp["L0_attn_bv_k"]),
        "bv": inp["L0_attn_bv_v"].reshape(H, HM, Q).transpose(0, 2, 1).reshape(1, D),
        "toep": toep.reshape(P, G, 2, P),
        "cw_t": inp["L0_cond2_c_weight"].T,
        "fside": inp["fside_S_0"].reshape(1, S),
        "a_t": inp["L0_ffn_A_w"].T.reshape(M, Q, NB),
        "wq": inp["L0_ffn_Wq_w"].reshape(RD, M, Q).transpose(0, 2, 1).reshape(RD, D),
        "keys_t": inp["L0_ffn_keys"].T,
        "b_t": inp["L0_ffn_B_w"].T.reshape(NT, P, M, Q).transpose(1, 0, 3, 2).reshape(P, NT, D),
    }
    arrays = {f"in_{k}": np.ascontiguousarray(v) for k, v in arrays.items()}
    nc = bacc.Bacc("TRN2", target_bir_lowering=False, num_devices=1)
    args = [nc.dram_tensor(k, v.shape, F32, kind="ExternalInput").ap() for k, v in arrays.items()]
    out = nc.dram_tensor("out", (B * S, D), F32, kind="ExternalOutput").ap()
    adaln_attn_ffn_kernel(nc, *args, out)
    r = run_bass_kernel_spmd(nc, [arrays], core_ids=[0])
    got = r.results[0]["out"]
    return got.reshape(B, S, Q, M).transpose(0, 1, 3, 2).reshape(B, S, D)
```

```python
from contextlib import ExitStack

import concourse.bass as bass
from concourse import mybir

F32 = mybir.dt.float32
F32R = mybir.dt.float32r
ALU = mybir.AluOpType
ACT = mybir.ActivationFunctionType
AX = mybir.AxisListType

B, S, D = 32, 64, 1024
P = 128
PAIRS = B // 2
H, HD = 4, 256
Q = 8
M = D // Q
HM = HD // Q
NK = 8
G, GC = 4, 16
TAPS, PAD = 9, 4
E, RANK, TOPK = 64, 8, 16
NB = E * RANK
RD = 16
NT = NB // P
ZW = (NB + E) // 2
XW = 132
SCALING = 2.0
LOWEST = -3.0e38
WARM = (3, 4, 0, 4, 1, 2, 4, 0, 0, 0)
CH = 4
CW = S * S // CH


PACK_P = {"emb_t": B, "w0": P, "w1": P, "w2": NK, "b0": 1, "b1": 1, "bq": 2 * H, "bk": 2 * H, "cw_t": S}
PACK_M = {"wk_t": CW, "wk_n": CW, "b2": NK, "fside": S, "bias_k": S}
PACK_R = {"wq": D, "keys_t": E}


def columns(pack):
    at, found = 0, {}
    for name, n in pack.items():
        found[name] = slice(at, at + n)
        at += n
    return found


def adaln_attn_ffn_kernel(nc, x, pack_p, pack_m, pack_r, bv, toep, a_t, b_t, out):
    ctx = ExitStack()
    with ctx:
        def sb(name, shape, dt=F32):
            return ctx.enter_context(nc.sbuf_tensor(name, shape, dt))

        def ps(name, shape):
            return ctx.enter_context(nc.psum_tensor(name, shape, F32))

        def sem(name):
            return ctx.enter_context(nc.semaphore(name))

        agg_n = nc.dram_tensor("agg_n", (B, S * S), F32, kind="Internal").ap()
        agg_t = nc.dram_tensor("agg_t", (B, S * S), F32, kind="Internal").ap()
        bias_d = nc.dram_tensor("bias_d", (B, 2 * S), F32, kind="Internal").ap()

        ident = sb("ident", [P, P])
        ones = sb("ones", [P, P])
        chunk_mask = sb("chunk_mask", [CH * NK, CH])
        mask_st = sb("mask_st", [P, S])
        mask_ts = sb("mask_ts", [P, S])
        a_raw = sb("a_raw", [P, Q, NB])
        b_raw = sb("b_raw", [P, NT, D])
        a_hi = sb("a_hi", [P, Q, NB + E], F32R)
        a_lo = sb("a_lo", [P, Q, NB + E], F32R)
        b_hi = sb("b_hi", [P, NT, D], F32R)
        b_lo = sb("b_lo", [P, NT, D], F32R)
        toep_sb = sb("toep_sb", [P, G, 2, P])
        vb = sb("vb", [P, H, HD])
        qk = sb("qk", [P, 2 * H])
        pp = sb("pp", [P, sum(PACK_P.values())])
        pm = sb("pm", [CH * NK, sum(PACK_M.values())])
        pr = sb("pr", [RD, sum(PACK_R.values())])
        cp, cm, cr = columns(PACK_P), columns(PACK_M), columns(PACK_R)
        bqk = pp[:, cp["bq"].start:cp["bk"].stop].rearrange("p (a t) -> p a t", a=2)
        h0 = sb("h0", [P, B])
        h1 = sb("h1", [P, B])
        lg = sb("lg", [B, 4, NK])
        lgs = sb("lgs", [B, 4])
        att_rep = sb("att_rep", [B, CH, NK])
        att4 = sb("att4", [CH * NK, CH, B])
        bias_sb = sb("bias_sb", [B, 2, S])
        bqk_t = sb("bqk_t", [P, 4, 2, 2 * H])
        bqk_a = sb("bqk_a", [P, 2, H])
        vraw = sb("vraw", [P, H, HD])
        valpha = sb("valpha", [P, 2, H])
        x_sb = [sb(f"x_sb{i}", [P, H, HD]) for i in range(2)]
        x1_sb = [sb(f"x1_sb{i}", [P, Q, XW]) for i in range(2)]
        wt_sb = [sb(f"wt_sb{i}", [P, P]) for i in range(2)]
        wn_sb = [sb(f"wn_sb{i}", [P, P]) for i in range(2)]
        bias_bc = [sb(f"bias_bc{i}", [P, 2, 2, S]) for i in range(2)]
        yT = sb("yT", [P, 2 * H, P])
        kT = sb("kT", [P, 2 * H, P])
        th = sb("th", [P, H, S])
        attnT = sb("attnT", [P, H, S])
        bm = sb("bm", [P, S])
        cprod = sb("cprod", [P, H, S])
        cvec = sb("cvec", [P, H])
        m_hi = sb("m_hi", [P, H, P], F32R)
        m_lo = sb("m_lo", [P, H, P], F32R)
        x_hi = sb("x_hi", [P, H, HD], F32R)
        x_lo = sb("x_lo", [P, H, HD], F32R)
        r_sb = sb("r_sb", [P, H, HD])
        xg = sb("xg", [P, 2, G, XW])
        c_sb = sb("c_sb", [P, Q, P])
        c_hi = sb("c_hi", [P, Q, P], F32R)
        c_lo = sb("c_lo", [P, Q, P], F32R)
        rs = sb("rs", [P, 6, E])
        gate = sb("gate", [P, 2, E])
        top8 = sb("top8", [P, 2, 8])
        gsum = sb("gsum", [P, 2])
        zg = sb("zg", [P, NB])
        zt_hi = sb("zt_hi", [P, NT, P], F32R)
        zt_lo = sb("zt_lo", [P, NT, P], F32R)
        o_sb = sb("o_sb", [P, 2, D // 2])
        agg_sb = [c_sb[:].rearrange("p q m -> p (q m)"), o_sb[:].rearrange("p j c -> p (j c)")]

        ps_y = [ps(f"ps_y{i}", [P, 512]) for i in range(2)]
        ps_c = [ps(f"ps_c{i}", [P, 512]) for i in range(2)]
        ps_z = [ps(f"ps_z{i}", [P, 512]) for i in range(2)]
        ps_s = ps("ps_s", [P, 512])
        ps_t = ps("ps_t", [P, 512])

        pp_in = sem("pp_in")
        pm_in = sem("pm_in")
        pr_in = sem("pr_in")
        bv_in = sem("bv_in")
        toep_in = sem("toep_in")
        a_in = sem("a_in")
        b_in = sem("b_in")
        const_step = sem("const_step")
        consts = sem("consts")
        cond_mm = sem("cond_mm")
        cond_act = sem("cond_act")
        cond_dve = sem("cond_dve")
        bind_dve = sem("bind_dve")
        bind_mm = sem("bind_mm")
        qk_abs = sem("qk_abs")
        v_abs = sem("v_abs")
        v_alpha = sem("v_alpha")
        v_step = sem("v_step")
        bias_out = sem("bias_out")
        scratch_out = sem("scratch_out")
        wqk_mm = sem("wqk_mm")
        split_hi = sem("split_hi")
        split_lo = sem("split_lo")
        x_in = [sem(f"x_in{i}") for i in range(2)]
        wt_in = [sem(f"wt_in{i}") for i in range(2)]
        wn_in = [sem(f"wn_in{i}") for i in range(2)]
        bias_in = [sem(f"bias_in{i}") for i in range(2)]
        y_mm = sem("y_mm")
        y_rdy = sem("y_rdy")
        k_rdy = sem("k_rdy")
        s_mm = sem("s_mm")
        th_rdy = sem("th_rdy")
        attn_rdy = sem("attn_rdy")
        c_step = sem("c_step")
        m_mm = sem("m_mm")
        m_rdy = sem("m_rdy")
        mlo_rdy = sem("mlo_rdy")
        xhi_rdy = sem("xhi_rdy")
        xlo_rdy = sem("xlo_rdy")
        ax_mm = sem("ax_mm")
        r_rdy = sem("r_rdy")
        x1_rdy = sem("x1_rdy")
        xg_in = [sem(f"xg_in{j}") for j in range(2)]
        c_mm = sem("c_mm")
        c_rdy = sem("c_rdy")
        chi_rdy = sem("chi_rdy")
        clo_rdy = sem("clo_rdy")
        z_mm = sem("z_mm")
        route = sem("route")
        bm_rdy = sem("bm_rdy")
        exp_rdy = sem("exp_rdy")
        gate_rdy = sem("gate_rdy")
        zg_rdy = sem("zg_rdy")
        t_mm = sem("t_mm")
        zhi_rdy = sem("zhi_rdy")
        zlo_rdy = sem("zlo_rdy")
        o_mm = sem("o_mm")
        o_rdy = sem("o_rdy")
        o_out = [sem(f"o_out{i}") for i in range(2)]
        ROUTE = 9

        def wait(eng, s, value):
            if not (isinstance(value, int) and value <= 0):
                eng.wait_ge(s, value)

        def number(pair):
            return pair[0] * 2 + pair[1]

        def is_first(pair):
            return pair is not None and isinstance(pair[0], int) and number(pair) == 0

        def run(eng, step):
            step((0, 0), None, None)
            step((0, 1), (0, 0), None)
            step((1, 0), (0, 1), (0, 0))
            step((1, 1), (1, 0), (0, 1))
            with eng.Fori(1, PAIRS // 2 - 1) as i:
                step((i + 1, 0), (i, 1), (i, 0))
                step((i + 1, 1), (i + 1, 0), (i, 1))
            last = PAIRS // 2 - 1
            step(None, (last, 1), (last, 0))
            step(None, None, (last, 1))

        block = ctx.enter_context(nc.Block())

        @block.sync
        def _(sp):
            def load_pair(pair):
                n, par = number(pair), pair[1]
                wait(sp, x1_rdy, n * 2 - 2)
                sp.dma_start(x_sb[par][:].rearrange("p h d -> p (h d)"),
                             x[bass.ds(n * P, P), :]).then_inc(x_in[par], 16)

            def load_weights(pair):
                n, par = number(pair), pair[1]
                wait(sp, m_mm, n - 1)
                for dst, src, done in ((wt_sb, agg_t, wt_in), (wn_sb, agg_n, wn_in)):
                    for j in range(2):
                        lo, hi = j * S, (j + 1) * S
                        sp.dma_start(dst[par][lo:hi, lo:hi],
                                     src[bass.ds(n * 2 + j, 1), :].rearrange("a (r c) -> (a r) c", c=S)
                                     ).then_inc(done[par], 16)

            def load_bias(pair):
                n, par = number(pair), pair[1]
                wait(sp, c_rdy, n * 2 - 2)
                sp.dma_start(bias_bc[par][:].rearrange("p b k s -> p (b k s)"),
                             bias_d[bass.ds(n * 2, 2), :].rearrange("(a b) s -> a (b s)", a=1)
                             .to_broadcast([P, 4 * S])).then_inc(bias_in[par], 16)

            def regroup(pair):
                n, par = number(pair), pair[1]
                wait(sp, x1_rdy, n * 2 + 2)
                wait(sp, c_mm, n * 2)
                for j in range(2):
                    for g in range(G):
                        lo = j * S + g * GC
                        sp.dma_start(xg[:, j, g, 0:M + 1],
                                     x1_sb[par][lo:lo + GC, :, 0:M + 1]).then_inc(xg_in[j], 16)

            def store(pair, j):
                n = number(pair)
                wait(sp, o_rdy, n * 2 + 1 + j)
                sp.dma_start(out[bass.ds(n * P, P), j * 512:(j + 1) * 512],
                             o_sb[:, j, :]).then_inc(o_out[j], 16)

            sp.dma_start(pp[:], pack_p).then_inc(pp_in, 16)
            load_pair((0, 0))
            sp.dma_start(vraw[:].rearrange("p h d -> p (h d)"), bv.to_broadcast([P, D])).then_inc(bv_in, 16)
            load_pair((0, 1))
            sp.dma_start(a_raw[:], a_t).then_inc(a_in, 16)
            sp.wait_ge(cond_dve, 8)
            sp.dma_start(bias_d, bias_sb[:].rearrange("b k s -> b (k s)")).then_inc(bias_out, 16)
            sp.wait_ge(consts, 1)
            for form, dst, done, acts, steps in ((0, wt_sb, wt_in, 4, 9), (1, wn_sb, wn_in, 5, 10)):
                sp.wait_ge(cond_act, acts)
                sp.wait_ge(cond_dve, steps)
                for b in range(4):
                    par, lo = b // 2, (b % 2) * S
                    sp.dma_start(dst[par][lo:lo + S, lo:lo + S],
                                 agg_sb[form][b:P:B, :]).then_inc(done[par], 16)
                if form == 0:
                    sp.wait_ge(bias_out, 16)
                    load_bias((0, 0))
                    load_bias((0, 1))
            sp.dma_start(toep_sb[:], toep).then_inc(toep_in, 16)
            sp.dma_start(b_raw[:], b_t).then_inc(b_in, 16)
            sp.wait_ge(cond_act, 5)
            sp.wait_ge(cond_dve, 10)
            for form, dram in ((0, agg_t), (1, agg_n)):
                for c in range(CH):
                    sp.dma_start(dram[:, c * CW:(c + 1) * CW],
                                 agg_sb[form][c * B:(c + 1) * B, :]).then_inc(scratch_out, 16)
            sp.wait_ge(scratch_out, 2 * CH * 16)

            def step(a, c, f):
                if f is not None and not is_first(f):
                    store((f[0], 0) if f[1] else (f[0] - 1, 1), 1)
                if c is not None:
                    regroup(c)
                nxt = after(a)
                if nxt is not None and not (isinstance(nxt[0], int) and number(nxt) < 2):
                    load_pair(nxt)
                    load_weights(nxt)
                    load_bias(nxt)
                if f is not None:
                    store(f, 0)

            def after(a):
                if a is None:
                    return None
                return (a[0], 1) if a[1] == 0 else (a[0] + 1, 0)

            step((0, 0), None, None)
            step((0, 1), (0, 0), None)
            step((1, 0), (0, 1), (0, 0))
            step((1, 1), (1, 0), (0, 1))
            with sp.Fori(1, PAIRS // 2 - 2) as i:
                step((i + 1, 0), (i, 1), (i, 0))
                step((i + 1, 1), (i + 1, 0), (i, 1))
            last = PAIRS // 2 - 1
            step((last, 0), (last - 1, 1), (last - 1, 0))
            step(None, (last, 0), (last - 1, 1))
            step(None, (last, 1), (last, 0))
            step(None, None, (last, 1))
            store((last, 1), 1)
            sp.wait_ge(o_out[0], PAIRS * 16)
            sp.wait_ge(o_out[1], PAIRS * 16)

        @block.gpsimd
        def _(pool):
            nc.gpsimd.memset(ident[:], 0.0).then_inc(const_step, 1)
            nc.gpsimd.memset(chunk_mask[:], 1.0).then_inc(const_step, 1)
            nc.gpsimd.memset(mask_st[:], 0.5).then_inc(const_step, 1)
            nc.gpsimd.memset(mask_ts[:], 0.5).then_inc(const_step, 1)
            nc.gpsimd.memset(ones[:], 1.0)
            pool.wait_ge(const_step, 4)
            nc.gpsimd.affine_select(out=ident[:], in_=ident[:], compare_op=ALU.not_equal, fill=1.0,
                                    base=0, pattern=[[-1, P]], channel_multiplier=1)
            nc.gpsimd.affine_select(out=chunk_mask[:], in_=chunk_mask[:], compare_op=ALU.is_ge, fill=0.0,
                                    base=0, pattern=[[-NK, CH]], channel_multiplier=1).then_inc(const_step, 1)
            pool.wait_ge(const_step, 5)
            nc.gpsimd.affine_select(out=chunk_mask[:], in_=chunk_mask[:], compare_op=ALU.is_ge, fill=0.0,
                                    base=NK - 1, pattern=[[NK, CH]], channel_multiplier=-1
                                    ).then_inc(const_step, 1)
            for j, lo in enumerate((0, S)):
                rows = slice(lo, lo + S)
                pool.wait_ge(const_step, 6 + 2 * j)
                nc.gpsimd.affine_select(out=mask_st[rows], in_=mask_st[rows], compare_op=ALU.is_ge, fill=0.0,
                                        base=0, pattern=[[1, S]], channel_multiplier=-1
                                        ).then_inc(const_step, 1)
                pool.wait_ge(const_step, 7 + 2 * j)
                last = nc.gpsimd.affine_select(out=mask_ts[rows], in_=mask_ts[rows], compare_op=ALU.is_ge,
                                               fill=0.0, base=0, pattern=[[-1, S]], channel_multiplier=1
                                               ).then_inc(const_step, 1)
            pool.wait_ge(const_step, 10)
            for i in range(2):
                nc.gpsimd.memset(wt_sb[i][:], 0.0)
                last = nc.gpsimd.memset(wn_sb[i][:], 0.0)
            last.then_inc(consts, 1)
            for i in range(2):
                last = nc.gpsimd.memset(x1_sb[i][:], 0.0)
            last.then_inc(const_step, 1)
            pool.wait_ge(const_step, 11)
            nc.gpsimd.tensor_copy(m_lo[:], x1_sb[1][:, 0:H, 0:P])
            nc.gpsimd.tensor_copy(m_hi[:], x1_sb[1][:, 0:H, 0:P]).then_inc(consts, 1)

            def bind_k(pair):
                n = number(pair)
                wait(pool, s_mm, n)
                for j in range(2):
                    wait(pool, y_rdy, n * 2 + 1 + j)
                    tiles = slice(4 * j, 4 * j + 4)
                    nc.gpsimd.tensor_tensor(kT[:, tiles], yT[:, tiles],
                                            qk[:, tiles].unsqueeze(2).to_broadcast([P, 4, P]),
                                            ALU.mult).then_inc(k_rdy, 1)

            def x_low(pair):
                n, par = number(pair), pair[1]
                wait(pool, xhi_rdy, n + 1)
                wait(pool, ax_mm, n * 2)
                nc.gpsimd.tensor_tensor(x_lo[:], x_sb[par][:], x_hi[:].bitcast(F32),
                                        ALU.subtract).then_inc(xlo_rdy, 1)

            def conv_low(pair):
                n = number(pair)
                wait(pool, chi_rdy, n + 1)
                nc.gpsimd.tensor_tensor(c_lo[:], c_sb[:], c_hi[:].bitcast(F32),
                                        ALU.subtract).then_inc(clo_rdy, 1)

            pool.wait_ge(v_step, 2)
            pool.wait_ge(v_alpha, 2)
            nc.gpsimd.tensor_tensor(vb[:], vb[:], valpha[:, 1, :].unsqueeze(2).to_broadcast([P, H, HD]),
                                    ALU.mult).then_inc(v_step, 1)
            pool.wait_ge(v_step, 3)
            nc.gpsimd.tensor_tensor(vb[:], vb[:], vraw[:], ALU.subtract).then_inc(v_step, 1)
            pool.wait_ge(v_step, 4)
            nc.gpsimd.tensor_tensor(vb[:], vb[:], vraw[:], ALU.add).then_inc(v_step, 1)
            pool.wait_ge(bind_dve, 8)
            pool.wait_ge(v_alpha, 1)
            def step(a, c, f):
                if a is not None:
                    bind_k(a)
                    x_low(a)
                if c is not None:
                    conv_low(c)

            run(pool, step)

        @block.scalar
        def _(act):
            act.dma_start(pm[:], pack_m).then_inc(pm_in, 16)
            act.dma_start(pr[:], pack_r).then_inc(pr_in, 16)
            act.wait_ge(pp_in, 16)
            act.wait_ge(cond_mm, 1)
            nc.scalar.activation(h0[:], ps_y[0][:, 0:B], ACT.Gelu, bias=pp[:, cp["b0"]]).then_inc(cond_act, 1)
            nc.scalar.activation(bqk_t[:, 0], bqk, ACT.Abs).then_inc(qk_abs, 1)
            act.wait_ge(cond_mm, 2)
            nc.scalar.activation(h1[:], ps_y[1][:, 0:B], ACT.Gelu, bias=pp[:, cp["b1"]]).then_inc(cond_act, 1)
            act.wait_ge(cond_dve, 3)
            nc.scalar.activation(lg[:, 2, :], lg[:, 1, :], ACT.Exp, accum_out=lgs[:, 1:2]).then_inc(cond_act, 1)
            act.wait_ge(bv_in, 16)
            nc.scalar.activation(kT[:].rearrange("p q m -> p (q m)"), vraw[:].rearrange("p h d -> p (h d)"),
                                 ACT.Abs).then_inc(v_abs, 1)
            for form, bank in ((0, ps_z), (1, ps_c)):
                act.wait_ge(cond_mm, 7 + 2 * form)
                nc.scalar.activation(agg_sb[form][:, 0:512], bank[0][:], ACT.Copy).then_inc(cond_act, 1)

            def split_weights():
                act.wait_ge(a_in, 16)
                nc.scalar.activation(a_hi[:, :, 0:NB], a_raw[:], ACT.Copy).then_inc(split_hi, 1)
                act.wait_ge(wqk_mm, 1)
                nc.scalar.activation(a_hi[:, :, NB:NB + E], ps_z[1][:].rearrange("p (q e) -> p q e", q=Q),
                                     ACT.Copy).then_inc(split_hi, 1)
                act.wait_ge(b_in, 16)
                nc.scalar.activation(b_hi[:], b_raw[:], ACT.Copy).then_inc(split_hi, 1)

            def x_high(pair):
                n, par = number(pair), pair[1]
                wait(act, x_in[par], pair[0] * 16 + 16)
                wait(act, ax_mm, n * 2)
                wait(act, xlo_rdy, n)
                nc.scalar.activation(x_hi[:], x_sb[par][:], ACT.Copy).then_inc(xhi_rdy, 1)

            def router_exp(pair):
                n = number(pair)
                wait(act, route, n * ROUTE + 2)
                nc.scalar.activation(rs[:, 4, :], rs[:, 3, :], ACT.Exp).then_inc(exp_rdy, 1)

            def scores_tanh(pair):
                n = number(pair)
                wait(act, s_mm, n + 1)
                wait(act, c_step, n * 2)
                for j in range(2):
                    rows = slice(j * S, (j + 1) * S)
                    nc.scalar.activation(th[rows], ps_s[rows].rearrange("p (h t) -> p h t", h=H)[:, :, rows],
                                         ACT.Tanh, scale=2.0 * HD ** -0.5).then_inc(th_rdy, 1)

            def m_out(pair):
                n = number(pair)
                wait(act, m_mm, n + 1)
                wait(act, ax_mm, n * 2)
                for j in range(2):
                    rows = slice(j * S, (j + 1) * S)
                    nc.scalar.activation(m_hi[rows, :, rows], ps_s[rows, 0:H * S]
                                         .rearrange("p (h t) -> p h t", h=H), ACT.Copy).then_inc(m_rdy, 1)

            def zt_high(pair):
                n = number(pair)
                wait(act, t_mm, n + 1)
                wait(act, o_mm, n * 2)
                nc.scalar.activation(zt_hi[:].rearrange("p a b -> p (a b)"), ps_t[:],
                                     ACT.Copy).then_inc(zhi_rdy, 1)

            def conv_high(pair):
                n = number(pair)
                wait(act, c_rdy, n * 2 + 2)
                wait(act, z_mm, n * 2)
                nc.scalar.activation(c_hi[:], c_sb[:], ACT.Copy).then_inc(chi_rdy, 1)

            def step(a, c, f):
                if a is not None:
                    x_high(a)
                if f is not None:
                    router_exp(f)
                if a is not None:
                    scores_tanh(a)
                    m_out(a)
                if is_first(a):
                    split_weights()
                if f is not None:
                    zt_high(f)
                if c is not None:
                    conv_high(c)

            run(act, step)

        @block.vector
        def _(dve):
            dve.wait_ge(pp_in, 16)
            dve.wait_ge(pm_in, 16)
            dve.wait_ge(cond_mm, 3)
            nc.vector.tensor_tensor(lg[:, 0, :], ps_c[0][0:B, 0:NK], pm[:, cm["b2"]], ALU.add).then_inc(cond_dve, 1)
            dve.wait_ge(cond_dve, 1)
            nc.vector.reduce_max(lgs[:, 0:1], lg[:, 0, :], AX.X).then_inc(cond_dve, 1)
            dve.wait_ge(cond_dve, 2)
            nc.vector.tensor_scalar(lg[:, 1, :], lg[:, 0, :], lgs[:, 0:1], None, ALU.subtract).then_inc(cond_dve, 1)
            dve.wait_ge(cond_act, 3)
            nc.vector.reciprocal(lgs[:, 2:3], lgs[:, 1:2]).then_inc(cond_dve, 1)
            dve.wait_ge(cond_dve, 4)
            nc.vector.tensor_scalar(att_rep[:], lg[:, 2:3, :].to_broadcast([B, CH, NK]),
                                    lgs[:, 2:3], None, ALU.mult).then_inc(cond_dve, 1)
            dve.wait_ge(cond_mm, 4)
            dve.wait_ge(const_step, 10)
            nc.vector.tensor_tensor(att4[:], ps_c[1][0:CH * NK, 0:B].unsqueeze(1).to_broadcast([CH * NK, CH, B]),
                                    chunk_mask[:].unsqueeze(2).to_broadcast([CH * NK, CH, B]),
                                    ALU.mult).then_inc(cond_dve, 1)
            dve.wait_ge(cond_mm, 6)
            dve.wait_ge(bind_mm, 1)
            nc.vector.tensor_copy(bias_sb[:, 0, :], ps_s[0:B, 0:S]).then_inc(cond_dve, 1)
            nc.vector.tensor_tensor(bias_sb[:, 1, :], ps_s[0:B, S:2 * S], pm[:, cm["fside"]],
                                    ALU.add).then_inc(cond_dve, 1)
            dve.wait_ge(v_abs, 1)
            nc.vector.tensor_reduce(valpha[:, 0, :],
                                    kT[:].rearrange("p (h j) c -> p h (j c)", h=H), AX.X, ALU.add).then_inc(v_alpha, 1)
            nc.vector.tensor_scalar(vb[:], vraw[:], 0.0, 2.0, ALU.is_ge, ALU.mult).then_inc(v_step, 1)
            dve.wait_ge(v_alpha, 1)
            nc.vector.tensor_scalar(valpha[:, 1, :], valpha[:, 0, :], 1.0 / HD, None, ALU.mult).then_inc(v_alpha, 1)
            dve.wait_ge(v_step, 1)
            nc.vector.tensor_scalar(vb[:], vb[:], -1.0, None, ALU.add).then_inc(v_step, 1)
            dve.wait_ge(cond_mm, 8)
            nc.vector.tensor_copy(agg_sb[0][:, 512:CW], ps_z[1][:]).then_inc(cond_dve, 1)
            nc.vector.reduce_sum(bqk_a[:], ps_s[:, 2 * S:2 * S + 4 * H].rearrange("p (a h j) -> p a h j", a=2, j=2),
                                 AX.X).then_inc(bind_dve, 1)
            nc.vector.tensor_scalar(bqk_t[:, 1], bqk, 0.0, 2.0, ALU.is_ge, ALU.mult).then_inc(bind_dve, 1)
            dve.wait_ge(bind_dve, 2)
            nc.vector.tensor_scalar(bqk_a[:], bqk_a[:], 1.0 / HD, None, ALU.mult).then_inc(bind_dve, 1)
            nc.vector.tensor_scalar(bqk_t[:, 1], bqk_t[:, 1], -1.0, None, ALU.add).then_inc(bind_dve, 1)
            dve.wait_ge(bind_dve, 4)
            nc.vector.tensor_tensor(bqk_t[:, 2].rearrange("p a (h j) -> p a h j", j=2),
                                    bqk_t[:, 1].rearrange("p a (h j) -> p a h j", j=2),
                                    bqk_a[:].unsqueeze(3).to_broadcast([P, 2, H, 2]), ALU.mult).then_inc(bind_dve, 1)
            dve.wait_ge(bind_dve, 5)
            nc.vector.tensor_tensor(bqk_t[:, 2], bqk_t[:, 2], bqk, ALU.subtract).then_inc(bind_dve, 1)
            dve.wait_ge(bind_dve, 6)
            nc.vector.tensor_tensor(bqk_t[:, 3], bqk_t[:, 2], bqk, ALU.add).then_inc(bind_dve, 1)
            dve.wait_ge(bind_dve, 7)
            nc.vector.tensor_tensor(qk[:], bqk_t[:, 3, 0, :], bqk_t[:, 3, 1, :], ALU.mult).then_inc(bind_dve, 1)
            dve.wait_ge(cond_mm, 10)
            nc.vector.tensor_copy(agg_sb[1][:, 512:CW], ps_c[1][:]).then_inc(cond_dve, 1)

            def split_a(half):
                if half == 0:
                    dve.wait_ge(split_hi, 2)
                    nc.vector.tensor_tensor(a_lo[:, :, NB:NB + E],
                                            ps_z[1][:].rearrange("p (q e) -> p q e", q=Q),
                                            a_hi[:, :, NB:NB + E].bitcast(F32), ALU.subtract).then_inc(split_lo, 1)
                ph = slice(half * Q // 2, (half + 1) * Q // 2)
                nc.vector.tensor_tensor(a_lo[:, ph, 0:NB], a_raw[:, ph], a_hi[:, ph, 0:NB].bitcast(F32),
                                        ALU.subtract).then_inc(split_lo, 1)

            def y_out(pair):
                n, par = number(pair), pair[1]
                wait(dve, s_mm, n)
                wait(dve, bias_in[par], pair[0] * 16 + 16)
                bias = bias_bc[par][:, :, 0, :].unsqueeze(1).to_broadcast([P, 4, 2, S])
                for j in range(2):
                    wait(dve, y_mm, n * 2 + 1 + j)
                    nc.vector.tensor_tensor(yT[:, 4 * j:4 * j + 4].rearrange("p a (b t) -> p a b t", b=2),
                                            ps_y[j][:].rearrange("p (a b t) -> p a b t", a=4, b=2),
                                            bias, ALU.add).then_inc(y_rdy, 1)

            def bias_mask(pair, j):
                par = pair[1]
                rows = slice(j * S, (j + 1) * S)
                nc.vector.tensor_tensor(bm[rows], mask_ts[rows], bias_bc[par][rows, j, 0, :],
                                        ALU.mult).then_inc(bm_rdy, 1)

            def router(a, f):
                n = number(f)
                at = lambda k: n * ROUTE + k
                scores = ps_z[1][:, ZW - E:ZW]
                wait(dve, z_mm, n * 2 + 1)
                nc.vector.tensor_copy(rs[:, 0, :], scores)
                nc.vector.max(top8[:, 0, :], scores).then_inc(route, 1)
                wait(dve, route, at(1))
                nc.vector.tensor_scalar(rs[:, 3, :], scores, top8[:, 0, 0:1], None,
                                        ALU.subtract).then_inc(route, 1)
                nc.vector.match_replace(rs[:, 1, :], top8[:, 0, :], scores, LOWEST).then_inc(route, 1)
                wait(dve, route, at(3))
                if a is not None:
                    bias_mask(a, 0)
                else:
                    nc.vector.tensor_copy(gate[:, 0, 0:1], top8[:, 0, 0:1])
                nc.vector.max(top8[:, 1, :], rs[:, 1, :]).then_inc(route, 1)
                wait(dve, route, at(4))
                if a is not None:
                    bias_mask(a, 1)
                else:
                    nc.vector.tensor_copy(gate[:, 0, 0:1], top8[:, 0, 0:1])
                nc.vector.match_replace(rs[:, 2, :], top8[:, 1, :], rs[:, 1, :], LOWEST).then_inc(route, 1)
                wait(dve, route, at(5))
                nc.vector.tensor_tensor(rs[:, 5, :], rs[:, 2, :], rs[:, 0, :], ALU.not_equal).then_inc(route, 1)
                wait(dve, exp_rdy, n + 1)
                wait(dve, route, at(6))
                nc.vector.tensor_tensor(gate[:, 0, :], rs[:, 4, :], rs[:, 5, :], ALU.mult).then_inc(route, 1)
                wait(dve, route, at(7))
                nc.vector.reduce_sum(gsum[:, 0:1], gate[:, 0, :], AX.X).then_inc(route, 1)
                wait(dve, route, at(8))
                nc.vector.reciprocal(gsum[:, 1:2], gsum[:, 0:1]).then_inc(route, 1)
                wait(dve, route, at(9))
                nc.vector.tensor_scalar(gate[:, 1, :], gate[:, 0, :], gsum[:, 1:2], SCALING,
                                        ALU.mult, ALU.mult).then_inc(gate_rdy, 1)
                wait(dve, gate_rdy, n + 1)
                wait(dve, t_mm, n)
                e0 = ZW // RANK
                for lo, hi, bank in ((e0, E, 1), (0, e0, 0)):
                    if bank == 0:
                        wait(dve, z_mm, n * 2 + 2)
                    nc.vector.tensor_tensor(
                        zg[:, lo * RANK:hi * RANK].rearrange("p (e r) -> p e r", r=RANK),
                        ps_z[bank][:, 0:(hi - lo) * RANK].rearrange("p (e r) -> p e r", r=RANK),
                        gate[:, 1, lo:hi].unsqueeze(2).to_broadcast([P, hi - lo, RANK]),
                        ALU.mult).then_inc(zg_rdy, 1)

            def masked(pair):
                n = number(pair)
                wait(dve, th_rdy, n * 2 + 2)
                wait(dve, m_mm, n)
                nc.vector.scalar_tensor_tensor(out=attnT[:], in0=th[:], scalar=1.0,
                                               in1=mask_st[:].unsqueeze(1).to_broadcast([P, H, S]),
                                               op0=ALU.add, op1=ALU.mult).then_inc(attn_rdy, 1)
                wait(dve, bm_rdy, n * 2 + 2)
                nc.vector.scalar_tensor_tensor(out=cprod[:], in0=th[:], scalar=1.0,
                                               in1=bm[:].unsqueeze(1).to_broadcast([P, H, S]),
                                               op0=ALU.add, op1=ALU.mult).then_inc(c_step, 1)
                wait(dve, c_step, n * 2 + 1)
                nc.vector.reduce_sum(cvec[:], cprod[:], AX.X).then_inc(c_step, 1)

            def conv_out(pair, j):
                n, par = number(pair), pair[1]
                wait(dve, chi_rdy, n)
                wait(dve, clo_rdy, n)
                wait(dve, c_mm, n * 2 + 1 + j)
                bias = bias_bc[par][:, j, 1, :].rearrange("p (g o) -> p g o", g=G)
                nc.vector.tensor_tensor(
                    c_sb[:, :, j * S:(j + 1) * S].rearrange("p r (g o) -> p r g o", g=G),
                    ps_c[j][:].rearrange("p (g r o) -> p r g o", g=G, r=Q),
                    bias.unsqueeze(1).to_broadcast([P, Q, G, GC]), ALU.add).then_inc(c_rdy, 1)

            def m_low(pair):
                n = number(pair)
                wait(dve, m_rdy, n * 2 + 2)
                wait(dve, ax_mm, n * 2)
                for j in range(2):
                    rows = slice(j * S, (j + 1) * S)
                    nc.vector.tensor_tensor(m_lo[rows, :, rows], ps_s[rows, 0:H * S]
                                            .rearrange("p (h t) -> p h t", h=H),
                                            m_hi[rows, :, rows].bitcast(F32), ALU.subtract).then_inc(mlo_rdy, 1)

            def zt_low(pair):
                n = number(pair)
                wait(dve, zhi_rdy, n + 1)
                wait(dve, o_mm, n * 2)
                nc.vector.tensor_tensor(zt_lo[:].rearrange("p a b -> p (a b)"), ps_t[:],
                                        zt_hi[:].bitcast(F32).rearrange("p a b -> p (a b)"),
                                        ALU.subtract).then_inc(zlo_rdy, 1)

            def attn_out(pair):
                n = number(pair)
                wait(dve, c_step, n * 2 + 2)
                for h in range(H):
                    if h % 2 == 0:
                        wait(dve, ax_mm, n * 2 + 1 + h // 2)
                    nc.vector.scalar_tensor_tensor(
                        out=r_sb[:, h, :], in0=ps_y[h // 2][:, (h % 2) * HD:(h % 2 + 1) * HD],
                        scalar=cvec[:, h:h + 1], in1=vb[:, h, :], op0=ALU.add, op1=ALU.mult).then_inc(r_rdy, 1)

            def residual(pair):
                n, par = number(pair), pair[1]
                wait(dve, r_rdy, n * 4 + 4)
                for j in range(2):
                    wait(dve, o_rdy, n * 2 - 3 + j)
                    ph = slice(4 * j, 4 * j + 4)
                    by_phase = lambda t: t[:].rearrange("p h (q m) -> p q h m", q=Q)[:, ph]
                    nc.vector.tensor_tensor(
                        x1_sb[par][:, ph, j:j + M].rearrange("p q (h m) -> p q h m", h=H),
                        by_phase(r_sb), by_phase(x_sb[par]), ALU.add).then_inc(x1_rdy, 1)

            def final(pair, j):
                n, par = number(pair), pair[1]
                wait(dve, o_mm, n * 2 + 1 + j)
                wait(dve, o_out[j], n * 16)
                nc.vector.tensor_tensor(o_sb[:, j, :].rearrange("p (q m) -> p q m", q=4),
                                        ps_z[j][:].rearrange("p (q m) -> p q m", q=4),
                                        x1_sb[par][:, 4 * j:4 * j + 4, j:j + M], ALU.add).then_inc(o_rdy, 1)

            def step(a, c, f):
                if f is not None and not is_first(f):
                    final((f[0], 0) if f[1] else (f[0] - 1, 1), 1)
                if is_first(c):
                    dve.wait_ge(consts, 2)
                if c is not None:
                    residual(c)
                if a is not None:
                    y_out(a)
                if is_first(f):
                    dve.wait_ge(split_hi, 3)
                    nc.vector.tensor_tensor(b_lo[:], b_raw[:], b_hi[:].bitcast(F32),
                                            ALU.subtract).then_inc(split_lo, 1)
                if f is not None:
                    router(a, f)
                elif a is not None:
                    bias_mask(a, 0)
                    bias_mask(a, 1)
                if is_first(c):
                    split_a(0)
                if a is not None:
                    masked(a)
                if is_first(c):
                    split_a(1)
                if is_first(c):
                    dve.wait_ge(scratch_out, 2 * CH * 16)
                    dve.wait_ge(wt_in[1], 32)
                    dve.wait_ge(wn_in[1], 32)
                if c is not None:
                    conv_out(c, 0)
                if is_first(a):
                    dve.wait_ge(consts, 2)
                if a is not None:
                    m_low(a)
                if f is not None:
                    zt_low(f)
                if c is not None:
                    conv_out(c, 1)
                if a is not None:
                    if is_first(a):
                        dve.wait_ge(v_step, 5)
                    attn_out(a)
                if f is not None:
                    final(f, 0)

            run(dve, step)
            final((PAIRS // 2 - 1, 1), 1)

        @block.tensor
        def _(pe):
            def keep_busy(products):
                for _ in range(products):
                    nc.tensor.matmul(ps_t[:, P:2 * P], ones[:], ones[:], start=True, stop=True)

            emb = pp[:, cp["emb_t"]]
            pe.wait_ge(const_step, 5)
            keep_busy(WARM[0])
            pe.wait_ge(pp_in, 16)
            nc.tensor.matmul(ps_y[0][:, 0:B], pp[:, cp["w0"]], emb, start=True, stop=True).then_inc(cond_mm, 1)
            keep_busy(WARM[1])
            pe.wait_ge(cond_act, 1)
            nc.tensor.matmul(ps_y[1][:, 0:B], pp[:, cp["w1"]], h0[:], start=True, stop=True).then_inc(cond_mm, 1)
            keep_busy(WARM[2])
            pe.wait_ge(cond_act, 2)
            nc.tensor.matmul(ps_c[0][0:B, 0:NK], h1[:], pp[:, cp["w2"]], start=True, stop=True).then_inc(cond_mm, 1)
            keep_busy(WARM[3])
            pe.wait_ge(cond_dve, 5)
            pe.wait_ge(const_step, 6)
            nc.tensor.matmul(ps_c[1][0:CH * NK, 0:B], att_rep[:].rearrange("b c k -> b (c k)"),
                             ident[0:B, 0:B], start=True, stop=True).then_inc(cond_mm, 1)
            pe.wait_ge(pm_in, 16)
            keep_busy(WARM[4])
            pe.wait_ge(const_step, 10)
            pe.wait_ge(qk_abs, 1)
            nc.tensor.matmul(ps_s[:, 2 * S:2 * S + 4 * H], ones[:], bqk_t[:, 0].rearrange("p a t -> p (a t)"),
                             start=True, stop=True).then_inc(bind_mm, 1)
            pe.wait_ge(cond_dve, 6)
            nc.tensor.matmul(ps_s[0:B, 0:S], att4[0:NK, 0, :], pm[0:NK, cm["bias_k"]],
                             start=True, stop=True).then_inc(cond_mm, 1)
            nc.tensor.matmul(ps_s[0:B, S:2 * S], emb, pp[:, cp["cw_t"]], start=True, stop=True).then_inc(cond_mm, 1)
            for form, bank in (("wk_t", ps_z), ("wk_n", ps_c)):
                for j in range(2):
                    at = cm[form].start + j * 512
                    nc.tensor.matmul(bank[j][:], att4[:].rearrange("r c b -> r (c b)"),
                                     pm[:, at:at + 512], start=True, stop=True).then_inc(cond_mm, 1)

            keep_busy(WARM[5])
            def router_weights():
                pe.wait_ge(pr_in, 16)
                pe.wait_ge(cond_dve, 9)
                for q in range(Q):
                    last = nc.tensor.matmul(ps_z[1][:, q * E:(q + 1) * E], pr[:, q * M:(q + 1) * M],
                                            pr[:, cr["keys_t"]], start=True, stop=True)
                last.then_inc(wqk_mm, 1)

            def y_product(pair):
                n, par = number(pair), pair[1]
                wait(pe, x_in[par], pair[0] * 16 + 16)
                wait(pe, wt_in[par], pair[0] * 32 + 32)
                for j in range(2):
                    wait(pe, r_rdy, n * 4 - 2 + 2 * j)
                    for k in range(4):
                        h, half = 2 * j + k // 2, k % 2
                        last = nc.tensor.matmul(ps_y[j][:, k * P:(k + 1) * P],
                                                x_sb[par][:, h, half * P:(half + 1) * P],
                                                wt_sb[par][:], start=True, stop=True)
                    last.then_inc(y_mm, 1)

            def scores(pair):
                n = number(pair)
                wait(pe, mlo_rdy, n * 2)
                for h in range(H):
                    if h % 2 == 0:
                        wait(pe, k_rdy, n * 2 + 1 + h // 2)
                    for k in range(2):
                        last = nc.tensor.matmul(ps_s[:, h * P:(h + 1) * P], kT[:, 2 * h + k, :],
                                                yT[:, 2 * h + k, :], start=(k == 0), stop=(k == 1))
                last.then_inc(s_mm, 1)

            def m_product(pair):
                n, par = number(pair), pair[1]
                wait(pe, wn_in[par], pair[0] * 32 + 32)
                wait(pe, attn_rdy, n + 1)
                nc.tensor.matmul(ps_s[:, 0:H * S], wn_sb[par][:], attnT[:].rearrange("p h t -> p (h t)"),
                                 start=True, stop=True).then_inc(m_mm, 1)

            def attn_x(pair):
                n = number(pair)
                wait(pe, xlo_rdy, n + 1)
                wait(pe, mlo_rdy, n * 2 + 2)
                for h in range(H):
                    for i, (w, m) in enumerate(((m_hi, x_hi), (m_hi, x_lo), (m_lo, x_hi))):
                        last = nc.tensor.matmul(ps_y[h // 2][:, (h % 2) * HD:(h % 2 + 1) * HD], w[:, h, :],
                                                m[:, h, :], start=(i == 0), stop=(i == 2))
                    if h % 2:
                        last.then_inc(ax_mm, 1)

            def conv(pair, first, end):
                n = number(pair)
                for jg in range(first, end):
                    j, g = jg // G, jg % G
                    if g == 0:
                        wait(pe, xg_in[j], (n + 1) * G * 16)
                        wait(pe, c_rdy, n * 2 - 1 + j)
                    for k in range(2):
                        last = nc.tensor.matmul(ps_c[j][:, g * P:(g + 1) * P], xg[:, j, g, k:k + M],
                                                toep_sb[:, g, k, :], start=(k == 0), stop=(k == 1))
                    if g == G - 1:
                        last.then_inc(c_mm, 1)

            def z_product(pair):
                n = number(pair)
                wait(pe, clo_rdy, n + 1)
                wait(pe, o_rdy, n * 2)
                for j in (1, 0):
                    for q in range(Q):
                        for i, (w, m) in enumerate(((c_hi, a_hi), (c_hi, a_lo), (c_lo, a_hi))):
                            last = nc.tensor.matmul(ps_z[j][:, 0:ZW], w[:, q, :], m[:, q, j * ZW:(j + 1) * ZW],
                                                    start=(q == 0 and i == 0), stop=(q == Q - 1 and i == 2))
                    last.then_inc(z_mm, 1)

            def turn(pair):
                n = number(pair)
                wait(pe, zg_rdy, n * 2 + 2)
                wait(pe, zlo_rdy, n)
                for k in range(NT):
                    last = nc.tensor.transpose(ps_t[:, k * P:(k + 1) * P], zg[:, k * P:(k + 1) * P], ident[:])
                last.then_inc(t_mm, 1)

            def out_product(pair, j):
                n = number(pair)
                if j == 0:
                    wait(pe, zlo_rdy, n + 1)
                cols = slice(j * 512, (j + 1) * 512)
                for k in range(NT):
                    for i, (w, m) in enumerate(((zt_hi, b_hi), (zt_hi, b_lo), (zt_lo, b_hi))):
                        last = nc.tensor.matmul(ps_z[j][:], w[:, k, :], m[:, k, cols],
                                                start=(k == 0 and i == 0), stop=(k == NT - 1 and i == 2))
                last.then_inc(o_mm, 1)

            def step(a, c, f):
                if a is not None:
                    y_product(a)
                if is_first(f):
                    pe.wait_ge(split_lo, 3)
                if f is not None:
                    z_product(f)
                if is_first(a):
                    keep_busy(WARM[6])
                if is_first(c):
                    keep_busy(WARM[7])
                if a is not None:
                    scores(a)
                if is_first(a):
                    router_weights()
                    keep_busy(WARM[8])
                if is_first(c):
                    pe.wait_ge(toep_in, 16)
                if c is not None:
                    conv(c, 0, G)
                if a is not None:
                    m_product(a)
                if f is not None:
                    turn(f)
                if is_first(a):
                    keep_busy(WARM[9])
                if c is not None:
                    conv(c, G, 2 * G)
                if a is not None:
                    if is_first(a):
                        pe.wait_ge(consts, 2)
                    attn_x(a)
                if is_first(f):
                    pe.wait_ge(split_lo, 4)
                if f is not None:
                    out_product(f, 0)
                    out_product(f, 1)

            run(pe, step)


def kernel(**inputs):
    import numpy as np
    import concourse.bacc as bacc
    from concourse.bass_utils import run_bass_kernel_spmd

    inp = {k: np.asarray(v) for k, v in inputs.items()}
    x = inp["x"].reshape(B * S, H, HM, Q).transpose(0, 1, 3, 2).reshape(B * S, D)
    wk = inp["L0_cond_weight"][..., 0]

    def chunks(w):
        return w.reshape(NK, CH, CW).transpose(1, 0, 2).reshape(CH * NK, CW)

    def tile_columns(w):
        return w.reshape(H, HM, 2, 4).transpose(3, 1, 0, 2).reshape(P, 2 * H)

    w = inp["L0_cond2_weight"].reshape(G, GC, GC, TAPS)
    toep = np.zeros((GC, Q, G, 2, Q, GC), w.dtype)
    for q in range(Q):
        p = q + PAD if q < PAD else q - PAD
        for k in range(2):
            for r in range(Q):
                tap = p + Q * k - r
                if 0 <= tap < TAPS:
                    toep[:, q, :, k, r, :] = w[:, :, :, tap].transpose(2, 0, 1)
    small = {
        "emb_t": inp["cond_128"].T,
        "w0": inp["L0_cond_W0"], "b0": inp["L0_cond_b0"].reshape(P, 1),
        "w1": inp["L0_cond_W1"], "b1": inp["L0_cond_b1"].reshape(P, 1),
        "w2": inp["L0_cond_W2"], "b2": np.broadcast_to(inp["L0_cond_b2"], (B, NK)),
        "wk_n": chunks(wk.reshape(NK, S * S)),
        "wk_t": chunks(wk.transpose(0, 2, 1).reshape(NK, S * S)),
        "bias_k": inp["L0_cond_bias_k"],
        "bq": tile_columns(inp["L0_attn_bv_q"]),
        "bk": tile_columns(inp["L0_attn_bv_k"]),
        "cw_t": inp["L0_cond2_c_weight"].T,
        "fside": np.broadcast_to(inp["fside_S_0"], (B, S)),
        "wq": inp["L0_ffn_Wq_w"].reshape(RD, M, Q).transpose(0, 2, 1).reshape(RD, D),
        "keys_t": inp["L0_ffn_keys"].T,
    }

    def pack(names, rows):
        packed = np.zeros((rows, sum(names.values())), np.float32)
        for name, cols in columns(names).items():
            packed[:small[name].shape[0], cols] = small[name]
        return packed

    arrays = {
        "x": x,
        "pack_p": pack(PACK_P, P),
        "pack_m": pack(PACK_M, CH * NK),
        "pack_r": pack(PACK_R, RD),
        "bv": inp["L0_attn_bv_v"].reshape(H, HM, Q).transpose(0, 2, 1).reshape(1, D),
        "toep": toep.reshape(P, G, 2, P),
        "a_t": inp["L0_ffn_A_w"].T.reshape(M, Q, NB),
        "b_t": inp["L0_ffn_B_w"].T.reshape(NT, P, M, Q).transpose(1, 0, 3, 2).reshape(P, NT, D),
    }
    arrays = {f"in_{k}": np.ascontiguousarray(v) for k, v in arrays.items()}
    nc = bacc.Bacc("TRN2", target_bir_lowering=False, num_devices=1)
    args = [nc.dram_tensor(k, v.shape, F32, kind="ExternalInput").ap() for k, v in arrays.items()]
    out = nc.dram_tensor("out", (B * S, D), F32, kind="ExternalOutput").ap()
    adaln_attn_ffn_kernel(nc, *args, out)
    r = run_bass_kernel_spmd(nc, [arrays], core_ids=[0])
    got = r.results[0]["out"]
    return got.reshape(B, S, Q, M).transpose(0, 1, 3, 2).reshape(B, S, D)
```

```python
from contextlib import ExitStack

import concourse.bass as bass
from concourse import mybir

F32 = mybir.dt.float32
F32R = mybir.dt.float32r
ALU = mybir.AluOpType
ACT = mybir.ActivationFunctionType
AX = mybir.AxisListType

B, S, D = 32, 64, 1024
P = 128
PAIRS = B // 2
H, HD = 4, 256
Q = 8
M = D // Q
HM = HD // Q
NK = 8
G, GC = 4, 16
TAPS, PAD = 9, 4
E, RANK, TOPK = 64, 8, 16
NB = E * RANK
RD = 16
NT = NB // P
ZW = (NB + RD) // 2
XW = 132
SCALING = 2.0
LOWEST = -3.0e38
FILL = (6, 4)
ROUTER_AT = (1, 4)
CH = 4
CW = S * S // CH


PACK_P = {"emb_t": B, "w0": P, "w1": P, "w2": NK, "b0": 1, "b1": 1, "bq": 2 * H, "bk": 2 * H, "cw_t": S}
PACK_M = {"wk_t": CW, "wk_n": CW, "b2": NK, "fside": S, "bias_k": S, "keys_t": E}


def columns(pack):
    at, found = 0, {}
    for name, n in pack.items():
        found[name] = slice(at, at + n)
        at += n
    return found


def adaln_attn_ffn_kernel(nc, x, pack_p, pack_m, bv, toep, a_t, b_t, out):
    ctx = ExitStack()
    with ctx:
        def sb(name, shape, dt=F32):
            return ctx.enter_context(nc.sbuf_tensor(name, shape, dt))

        def ps(name, shape):
            return ctx.enter_context(nc.psum_tensor(name, shape, F32))

        def sem(name):
            return ctx.enter_context(nc.semaphore(name))

        agg_n = nc.dram_tensor("agg_n", (B, S * S), F32, kind="Internal").ap()
        agg_t = nc.dram_tensor("agg_t", (B, S * S), F32, kind="Internal").ap()
        bias_d = nc.dram_tensor("bias_d", (B, 2 * S), F32, kind="Internal").ap()

        ident = sb("ident", [P, P])
        ones = sb("ones", [P, P])
        chunk_mask = sb("chunk_mask", [CH * NK, CH])
        mask_st = sb("mask_st", [P, S])
        mask_ts = sb("mask_ts", [P, S])
        a_raw = sb("a_raw", [P, Q, NB + RD])
        b_raw = sb("b_raw", [P, NT, D])
        a_hi = sb("a_hi", [P, Q, NB + RD], F32R)
        a_lo = sb("a_lo", [P, Q, NB + RD], F32R)
        b_hi = sb("b_hi", [P, NT, D], F32R)
        b_lo = sb("b_lo", [P, NT, D], F32R)
        toep_sb = sb("toep_sb", [P, G, 2, P])
        vb = sb("vb", [P, H, HD])
        qk = sb("qk", [P, 2 * H])
        pp = sb("pp", [P, sum(PACK_P.values())])
        pm = sb("pm", [CH * NK, sum(PACK_M.values())])
        cp, cm = columns(PACK_P), columns(PACK_M)
        bqk = pp[:, cp["bq"].start:cp["bk"].stop].rearrange("p (a t) -> p a t", a=2)
        h0 = sb("h0", [P, B])
        h1 = sb("h1", [P, B])
        lg = sb("lg", [B, 4, NK])
        lgs = sb("lgs", [B, 4])
        att_rep = sb("att_rep", [B, CH, NK])
        att4 = sb("att4", [CH * NK, CH, B])
        bias_sb = sb("bias_sb", [B, 2, S])
        bqk_t = sb("bqk_t", [P, 4, 2, 2 * H])
        bqk_a = sb("bqk_a", [P, 2, H])
        vraw = sb("vraw", [P, H, HD])
        valpha = sb("valpha", [P, 2, H])
        x_sb = [sb(f"x_sb{i}", [P, H, HD]) for i in range(2)]
        x1_sb = [sb(f"x1_sb{i}", [P, Q, XW]) for i in range(2)]
        wt_sb = [sb(f"wt_sb{i}", [P, P]) for i in range(2)]
        wn_sb = [sb(f"wn_sb{i}", [P, P]) for i in range(2)]
        bias_bc = [sb(f"bias_bc{i}", [P, 2, 2, S]) for i in range(2)]
        yT = sb("yT", [P, 2 * H, P])
        kT = sb("kT", [P, 2 * H, P])
        th = sb("th", [P, H, S])
        attnT = sb("attnT", [P, H, S])
        bm = sb("bm", [P, S])
        cprod = sb("cprod", [P, H, S])
        cvec = sb("cvec", [P, H])
        m_hi = sb("m_hi", [P, H, P], F32R)
        m_lo = sb("m_lo", [P, H, P], F32R)
        x_hi = sb("x_hi", [P, H, HD], F32R)
        x_lo = sb("x_lo", [P, H, HD], F32R)
        r_sb = sb("r_sb", [P, H, HD])
        xg = sb("xg", [P, 2, G, XW])
        c_sb = sb("c_sb", [P, Q, P])
        c_hi = sb("c_hi", [P, Q, P], F32R)
        c_lo = sb("c_lo", [P, Q, P], F32R)
        rs = sb("rs", [P, 6, E])
        q_sb = sb("q_sb", [P, RD])
        qT_sb = sb("qT_sb", [RD, P])
        gate = sb("gate", [P, 2, E])
        top8 = sb("top8", [P, 2, 8])
        gsum = sb("gsum", [P, 2])
        zg = sb("zg", [P, NB])
        zt_hi = sb("zt_hi", [P, NT, P], F32R)
        zt_lo = sb("zt_lo", [P, NT, P], F32R)
        o_sb = sb("o_sb", [P, 2, D // 2])
        agg_sb = [c_sb[:].rearrange("p q m -> p (q m)"), o_sb[:].rearrange("p j c -> p (j c)")]

        ps_y = [ps(f"ps_y{i}", [P, 512]) for i in range(2)]
        ps_c = [ps(f"ps_c{i}", [P, 512]) for i in range(2)]
        ps_z = [ps(f"ps_z{i}", [P, 512]) for i in range(2)]
        ps_s = ps("ps_s", [P, 512])
        ps_t = ps("ps_t", [P, 512])

        pp_in = sem("pp_in")
        pm_in = sem("pm_in")
        bv_in = sem("bv_in")
        toep_in = sem("toep_in")
        a_in = sem("a_in")
        b_in = sem("b_in")
        const_step = sem("const_step")
        consts = sem("consts")
        cond_mm = sem("cond_mm")
        cond_act = sem("cond_act")
        cond_dve = sem("cond_dve")
        bind_dve = sem("bind_dve")
        bind_mm = sem("bind_mm")
        qk_abs = sem("qk_abs")
        v_abs = sem("v_abs")
        v_alpha = sem("v_alpha")
        v_step = sem("v_step")
        bias_out = sem("bias_out")
        scratch_out = sem("scratch_out")
        split_hi = sem("split_hi")
        split_lo_pool = sem("split_lo_pool")
        split_lo = sem("split_lo")
        x_in = [sem(f"x_in{i}") for i in range(2)]
        wt_in = [sem(f"wt_in{i}") for i in range(2)]
        wn_in = [sem(f"wn_in{i}") for i in range(2)]
        bias_in = [sem(f"bias_in{i}") for i in range(2)]
        y_mm = sem("y_mm")
        y_rdy = sem("y_rdy")
        k_rdy = sem("k_rdy")
        s_mm = sem("s_mm")
        th_rdy = sem("th_rdy")
        attn_rdy = sem("attn_rdy")
        c_step = sem("c_step")
        m_mm = sem("m_mm")
        m_rdy = sem("m_rdy")
        mlo_rdy = sem("mlo_rdy")
        xhi_rdy = sem("xhi_rdy")
        xlo_rdy = sem("xlo_rdy")
        ax_mm = sem("ax_mm")
        r_rdy = sem("r_rdy")
        x1_rdy = sem("x1_rdy")
        xg_in = [sem(f"xg_in{jg}") for jg in range(2 * G)]
        c_mm = sem("c_mm")
        c_rdy = sem("c_rdy")
        chi_rdy = sem("chi_rdy")
        clo_rdy = sem("clo_rdy")
        z_mm = sem("z_mm")
        q_rdy = sem("q_rdy")
        q_mm = sem("q_mm")
        qT_rdy = sem("qT_rdy")
        rs_mm = sem("rs_mm")
        route = sem("route")
        bm_rdy = sem("bm_rdy")
        exp_rdy = sem("exp_rdy")
        gate_rdy = sem("gate_rdy")
        zg_rdy = sem("zg_rdy")
        t_mm = sem("t_mm")
        zhi_rdy = sem("zhi_rdy")
        zlo_rdy = sem("zlo_rdy")
        o_mm = sem("o_mm")
        o_rdy = sem("o_rdy")
        o_out = [sem(f"o_out{i}") for i in range(2)]
        ROUTE = 9

        def wait(eng, s, value):
            if not (isinstance(value, int) and value <= 0):
                eng.wait_ge(s, value)

        def number(pair):
            return pair[0] * 2 + pair[1]

        def is_first(pair):
            return pair is not None and isinstance(pair[0], int) and number(pair) == 0

        def is_second(pair):
            return pair is not None and isinstance(pair[0], int) and number(pair) == 1

        def is_last(pair):
            return pair is not None and isinstance(pair[0], int) and number(pair) == PAIRS - 1

        def z_banks(pair):
            return (ps_y[1], ps_y[0]) if is_last(pair) else (ps_z[1], ps_z[0])

        def y_banks(pair):
            return (ps_z[0], ps_z[1]) if is_second(pair) else (ps_y[0], ps_y[1])

        def run(eng, step):
            step((0, 0), None, None)
            step((0, 1), (0, 0), None)
            step((1, 0), (0, 1), (0, 0))
            step((1, 1), (1, 0), (0, 1))
            with eng.Fori(1, PAIRS // 2 - 1) as i:
                step((i + 1, 0), (i, 1), (i, 0))
                step((i + 1, 1), (i + 1, 0), (i, 1))
            last = PAIRS // 2 - 1
            step(None, (last, 1), (last, 0))
            step(None, None, (last, 1))

        block = ctx.enter_context(nc.Block())

        @block.sync
        def _(sp):
            def load_pair(pair):
                n, par = number(pair), pair[1]
                wait(sp, x1_rdy, n * 2 - 2)
                sp.dma_start(x_sb[par][:].rearrange("p h d -> p (h d)"),
                             x[bass.ds(n * P, P), :]).then_inc(x_in[par], 16)

            def load_weights(pair):
                n, par = number(pair), pair[1]
                wait(sp, m_mm, n - 1)
                for dst, src, done in ((wt_sb, agg_t, wt_in), (wn_sb, agg_n, wn_in)):
                    for j in range(2):
                        lo, hi = j * S, (j + 1) * S
                        sp.dma_start(dst[par][lo:hi, lo:hi],
                                     src[bass.ds(n * 2 + j, 1), :].rearrange("a (r c) -> (a r) c", c=S)
                                     ).then_inc(done[par], 16)

            def load_bias(pair):
                n, par = number(pair), pair[1]
                wait(sp, c_rdy, n * 2 - 2)
                sp.dma_start(bias_bc[par][:].rearrange("p b k s -> p (b k s)"),
                             bias_d[bass.ds(n * 2, 2), :].rearrange("(a b) s -> a (b s)", a=1)
                             .to_broadcast([P, 4 * S])).then_inc(bias_in[par], 16)

            def regroup(pair):
                n, par = number(pair), pair[1]
                wait(sp, x1_rdy, n * 2 + 2)
                wait(sp, c_mm, n * 2)
                for j in range(2):
                    for g in range(G):
                        lo = j * S + g * GC
                        sp.dma_start(xg[:, j, g, 0:M + 1],
                                     x1_sb[par][lo:lo + GC, :, 0:M + 1]).then_inc(xg_in[j * G + g], 16)

            def store(pair, j):
                n = number(pair)
                wait(sp, o_rdy, n * 2 + 1 + j)
                sp.dma_start(out[bass.ds(n * P, P), j * 512:(j + 1) * 512],
                             o_sb[:, j, :]).then_inc(o_out[j], 16)

            sp.dma_start(pp[:], pack_p).then_inc(pp_in, 16)
            load_pair((0, 0))
            sp.dma_start(vraw[:].rearrange("p h d -> p (h d)"), bv.to_broadcast([P, D])).then_inc(bv_in, 16)
            load_pair((0, 1))
            sp.dma_start(a_raw[:], a_t).then_inc(a_in, 16)
            sp.wait_ge(cond_dve, 8)
            sp.dma_start(bias_d, bias_sb[:].rearrange("b k s -> b (k s)")).then_inc(bias_out, 16)
            sp.wait_ge(consts, 1)
            for form, dst, done, acts, steps in ((0, wt_sb, wt_in, 4, 9), (1, wn_sb, wn_in, 5, 10)):
                sp.wait_ge(cond_act, acts)
                sp.wait_ge(cond_dve, steps)
                for b in range(4):
                    par, lo = b // 2, (b % 2) * S
                    sp.dma_start(dst[par][lo:lo + S, lo:lo + S],
                                 agg_sb[form][b:P:B, :]).then_inc(done[par], 16)
                if form == 0:
                    sp.wait_ge(bias_out, 16)
                    load_bias((0, 0))
                    load_bias((0, 1))
            sp.dma_start(toep_sb[:], toep).then_inc(toep_in, 16)
            sp.wait_ge(cond_act, 5)
            sp.wait_ge(cond_dve, 10)
            for form, dram in ((0, agg_t), (1, agg_n)):
                for c in range(CH):
                    sp.dma_start(dram[:, c * CW:(c + 1) * CW],
                                 agg_sb[form][c * B:(c + 1) * B, :]).then_inc(scratch_out, 16)
            sp.dma_start(b_raw[:], b_t).then_inc(b_in, 16)
            sp.wait_ge(scratch_out, 2 * CH * 16)

            def step(a, c, f):
                if f is not None and not is_first(f):
                    store((f[0], 0) if f[1] else (f[0] - 1, 1), 1)
                nxt = after(a)
                if nxt is not None and isinstance(nxt[0], int) and number(nxt) < 2:
                    nxt = None
                if nxt is not None:
                    load_weights(nxt)
                    load_pair(nxt)
                if c is not None:
                    regroup(c)
                if nxt is not None:
                    load_bias(nxt)
                if f is not None:
                    store(f, 0)

            def after(a):
                if a is None:
                    return None
                return (a[0], 1) if a[1] == 0 else (a[0] + 1, 0)

            step((0, 0), None, None)
            step((0, 1), (0, 0), None)
            step((1, 0), (0, 1), (0, 0))
            step((1, 1), (1, 0), (0, 1))
            with sp.Fori(1, PAIRS // 2 - 2) as i:
                step((i + 1, 0), (i, 1), (i, 0))
                step((i + 1, 1), (i + 1, 0), (i, 1))
            last = PAIRS // 2 - 1
            step((last, 0), (last - 1, 1), (last - 1, 0))
            step(None, (last, 0), (last - 1, 1))
            step(None, (last, 1), (last, 0))
            step(None, None, (last, 1))
            store((last, 1), 1)
            sp.wait_ge(o_out[0], PAIRS * 16)
            sp.wait_ge(o_out[1], PAIRS * 16)

        @block.gpsimd
        def _(pool):
            nc.gpsimd.memset(ident[:], 0.0).then_inc(const_step, 1)
            nc.gpsimd.memset(chunk_mask[:], 1.0).then_inc(const_step, 1)
            nc.gpsimd.memset(mask_st[:], 0.5).then_inc(const_step, 1)
            nc.gpsimd.memset(mask_ts[:], 0.5).then_inc(const_step, 1)
            nc.gpsimd.memset(ones[:], 1.0)
            pool.wait_ge(const_step, 4)
            nc.gpsimd.affine_select(out=ident[:], in_=ident[:], compare_op=ALU.not_equal, fill=1.0,
                                    base=0, pattern=[[-1, P]], channel_multiplier=1)
            nc.gpsimd.affine_select(out=chunk_mask[:], in_=chunk_mask[:], compare_op=ALU.is_ge, fill=0.0,
                                    base=0, pattern=[[-NK, CH]], channel_multiplier=1).then_inc(const_step, 1)
            pool.wait_ge(const_step, 5)
            nc.gpsimd.affine_select(out=chunk_mask[:], in_=chunk_mask[:], compare_op=ALU.is_ge, fill=0.0,
                                    base=NK - 1, pattern=[[NK, CH]], channel_multiplier=-1
                                    ).then_inc(const_step, 1)
            for j, lo in enumerate((0, S)):
                rows = slice(lo, lo + S)
                pool.wait_ge(const_step, 6 + 2 * j)
                nc.gpsimd.affine_select(out=mask_st[rows], in_=mask_st[rows], compare_op=ALU.is_ge, fill=0.0,
                                        base=0, pattern=[[1, S]], channel_multiplier=-1
                                        ).then_inc(const_step, 1)
                pool.wait_ge(const_step, 7 + 2 * j)
                last = nc.gpsimd.affine_select(out=mask_ts[rows], in_=mask_ts[rows], compare_op=ALU.is_ge,
                                               fill=0.0, base=0, pattern=[[-1, S]], channel_multiplier=1
                                               ).then_inc(const_step, 1)
            pool.wait_ge(const_step, 10)
            for i in range(2):
                nc.gpsimd.memset(wt_sb[i][:], 0.0)
                last = nc.gpsimd.memset(wn_sb[i][:], 0.0)
            last.then_inc(consts, 1)
            for i in range(2):
                last = nc.gpsimd.memset(x1_sb[i][:], 0.0)
            last.then_inc(const_step, 1)
            pool.wait_ge(const_step, 11)
            nc.gpsimd.tensor_copy(m_lo[:], x1_sb[1][:, 0:H, 0:P])
            nc.gpsimd.tensor_copy(m_hi[:], x1_sb[1][:, 0:H, 0:P]).then_inc(consts, 1)

            def bind_k(pair):
                n = number(pair)
                wait(pool, s_mm, n)
                for j in range(2):
                    wait(pool, y_rdy, n * 2 + 1 + j)
                    tiles = slice(4 * j, 4 * j + 4)
                    nc.gpsimd.tensor_tensor(kT[:, tiles], yT[:, tiles],
                                            qk[:, tiles].unsqueeze(2).to_broadcast([P, 4, P]),
                                            ALU.mult).then_inc(k_rdy, 1)

            def x_low(pair):
                n, par = number(pair), pair[1]
                wait(pool, xhi_rdy, n + 1)
                wait(pool, ax_mm, n * 2)
                nc.gpsimd.tensor_tensor(x_lo[:], x_sb[par][:], x_hi[:].bitcast(F32),
                                        ALU.subtract).then_inc(xlo_rdy, 1)

            def conv_low(pair):
                n = number(pair)
                wait(pool, chi_rdy, n + 1)
                nc.gpsimd.tensor_tensor(c_lo[:], c_sb[:], c_hi[:].bitcast(F32),
                                        ALU.subtract).then_inc(clo_rdy, 1)

            pool.wait_ge(v_step, 2)
            pool.wait_ge(v_alpha, 2)
            nc.gpsimd.tensor_tensor(vb[:], vb[:], valpha[:, 1, :].unsqueeze(2).to_broadcast([P, H, HD]),
                                    ALU.mult).then_inc(v_step, 1)
            pool.wait_ge(v_step, 3)
            nc.gpsimd.tensor_tensor(vb[:], vb[:], vraw[:], ALU.subtract).then_inc(v_step, 1)
            pool.wait_ge(v_step, 4)
            nc.gpsimd.tensor_tensor(vb[:], vb[:], vraw[:], ALU.add).then_inc(v_step, 1)
            pool.wait_ge(bind_dve, 8)
            pool.wait_ge(v_alpha, 1)
            def step(a, c, f):
                if a is not None and not is_second(a):
                    bind_k(a)
                if a is not None:
                    x_low(a)
                if is_first(a):
                    bind_k((0, 1))
                if is_second(a):
                    pool.wait_ge(split_hi, 1)
                    nc.gpsimd.tensor_tensor(a_lo[:, 0:Q // 2], a_raw[:, 0:Q // 2], a_hi[:, 0:Q // 2].bitcast(F32),
                                            ALU.subtract).then_inc(split_lo_pool, 1)
                if is_first(f):
                    pool.wait_ge(split_hi, 2)
                    nc.gpsimd.tensor_tensor(b_lo[:, 0:NT // 2], b_raw[:, 0:NT // 2], b_hi[:, 0:NT // 2].bitcast(F32),
                                            ALU.subtract).then_inc(split_lo_pool, 1)
                if c is not None:
                    conv_low(c)

            run(pool, step)

        @block.scalar
        def _(act):
            act.dma_start(pm[:], pack_m).then_inc(pm_in, 16)
            act.wait_ge(const_step, 5)
            nc.scalar.activation(th[:, 0, 0:1], ones[:, 0:1], ACT.Gelu)
            act.wait_ge(pp_in, 16)
            act.wait_ge(cond_mm, 1)
            nc.scalar.activation(h0[:], ps_y[0][:, 0:B], ACT.Gelu, bias=pp[:, cp["b0"]]).then_inc(cond_act, 1)
            nc.scalar.activation(bqk_t[:, 0], bqk, ACT.Abs).then_inc(qk_abs, 1)
            act.wait_ge(cond_mm, 2)
            nc.scalar.activation(h1[:], ps_y[1][:, 0:B], ACT.Gelu, bias=pp[:, cp["b1"]]).then_inc(cond_act, 1)
            act.wait_ge(cond_dve, 3)
            nc.scalar.activation(lg[:, 2, :], lg[:, 1, :], ACT.Exp, accum_out=lgs[:, 1:2]).then_inc(cond_act, 1)
            act.wait_ge(bv_in, 16)
            nc.scalar.activation(kT[:].rearrange("p q m -> p (q m)"), vraw[:].rearrange("p h d -> p (h d)"),
                                 ACT.Abs).then_inc(v_abs, 1)
            for form, bank in ((0, ps_z), (1, ps_c)):
                act.wait_ge(cond_mm, 7 + 2 * form)
                nc.scalar.activation(agg_sb[form][:, 0:512], bank[0][:], ACT.Copy).then_inc(cond_act, 1)

            def weights_high(loaded, raw, high):
                act.wait_ge(loaded, 16)
                nc.scalar.activation(high[:], raw[:], ACT.Copy).then_inc(split_hi, 1)

            def x_high(pair):
                n, par = number(pair), pair[1]
                wait(act, x_in[par], pair[0] * 16 + 16)
                wait(act, ax_mm, n * 2)
                wait(act, xlo_rdy, n)
                nc.scalar.activation(x_hi[:], x_sb[par][:], ACT.Copy).then_inc(xhi_rdy, 1)

            def query_out(pair):
                n = number(pair)
                wait(act, z_mm, n * 2 + 1)
                wait(act, q_mm, n)
                nc.scalar.activation(q_sb[:], z_banks(pair)[1][:, ZW - RD:ZW], ACT.Copy).then_inc(q_rdy, 1)
                wait(act, q_mm, n + 1)
                wait(act, rs_mm, n)
                nc.scalar.activation(qT_sb[:], ps_t[0:RD, 0:P], ACT.Copy).then_inc(qT_rdy, 1)

            def router_exp(pair):
                n = number(pair)
                wait(act, route, n * ROUTE + 2)
                nc.scalar.activation(rs[:, 4, :], rs[:, 3, :], ACT.Exp).then_inc(exp_rdy, 1)

            def scores_tanh(pair):
                n = number(pair)
                wait(act, s_mm, n + 1)
                wait(act, c_step, n * 2)
                for j in range(2):
                    rows = slice(j * S, (j + 1) * S)
                    nc.scalar.activation(th[rows], ps_s[rows].rearrange("p (h t) -> p h t", h=H)[:, :, rows],
                                         ACT.Tanh, scale=2.0 * HD ** -0.5).then_inc(th_rdy, 1)

            def m_out(pair):
                n = number(pair)
                wait(act, m_mm, n + 1)
                wait(act, ax_mm, n * 2)
                for j in range(2):
                    rows = slice(j * S, (j + 1) * S)
                    nc.scalar.activation(m_hi[rows, :, rows], ps_s[rows, 0:H * S]
                                         .rearrange("p (h t) -> p h t", h=H), ACT.Copy).then_inc(m_rdy, 1)

            def zt_high(pair):
                n = number(pair)
                wait(act, t_mm, n + 1)
                wait(act, o_mm, n * 2)
                nc.scalar.activation(zt_hi[:].rearrange("p a b -> p (a b)"), ps_t[:],
                                     ACT.Copy).then_inc(zhi_rdy, 1)

            def conv_high(pair):
                n = number(pair)
                wait(act, c_rdy, n * 2 + 2)
                wait(act, z_mm, n * 2)
                nc.scalar.activation(c_hi[:], c_sb[:], ACT.Copy).then_inc(chi_rdy, 1)

            def step(a, c, f):
                if a is not None:
                    x_high(a)
                if f is not None:
                    query_out(f)
                    router_exp(f)
                if a is not None:
                    scores_tanh(a)
                    m_out(a)
                if is_first(a):
                    weights_high(a_in, a_raw, a_hi)
                if is_second(a):
                    weights_high(b_in, b_raw, b_hi)
                if f is not None:
                    zt_high(f)
                if c is not None:
                    conv_high(c)

            run(act, step)

        @block.vector
        def _(dve):
            dve.wait_ge(pp_in, 16)
            dve.wait_ge(pm_in, 16)
            dve.wait_ge(cond_mm, 3)
            nc.vector.tensor_tensor(lg[:, 0, :], ps_c[0][0:B, 0:NK], pm[:, cm["b2"]], ALU.add).then_inc(cond_dve, 1)
            dve.wait_ge(cond_dve, 1)
            nc.vector.reduce_max(lgs[:, 0:1], lg[:, 0, :], AX.X).then_inc(cond_dve, 1)
            dve.wait_ge(cond_dve, 2)
            nc.vector.tensor_scalar(lg[:, 1, :], lg[:, 0, :], lgs[:, 0:1], None, ALU.subtract).then_inc(cond_dve, 1)
            dve.wait_ge(cond_act, 3)
            nc.vector.reciprocal(lgs[:, 2:3], lgs[:, 1:2]).then_inc(cond_dve, 1)
            dve.wait_ge(cond_dve, 4)
            nc.vector.tensor_scalar(att_rep[:], lg[:, 2:3, :].to_broadcast([B, CH, NK]),
                                    lgs[:, 2:3], None, ALU.mult).then_inc(cond_dve, 1)
            dve.wait_ge(cond_mm, 4)
            dve.wait_ge(const_step, 10)
            nc.vector.tensor_tensor(att4[:], ps_c[1][0:CH * NK, 0:B].unsqueeze(1).to_broadcast([CH * NK, CH, B]),
                                    chunk_mask[:].unsqueeze(2).to_broadcast([CH * NK, CH, B]),
                                    ALU.mult).then_inc(cond_dve, 1)
            dve.wait_ge(cond_mm, 6)
            dve.wait_ge(bind_mm, 1)
            nc.vector.tensor_copy(bias_sb[:, 0, :], ps_s[0:B, 0:S]).then_inc(cond_dve, 1)
            nc.vector.tensor_tensor(bias_sb[:, 1, :], ps_s[0:B, S:2 * S], pm[:, cm["fside"]],
                                    ALU.add).then_inc(cond_dve, 1)
            dve.wait_ge(v_abs, 1)
            nc.vector.tensor_reduce(valpha[:, 0, :],
                                    kT[:].rearrange("p (h j) c -> p h (j c)", h=H), AX.X, ALU.add).then_inc(v_alpha, 1)
            nc.vector.tensor_scalar(vb[:], vraw[:], 0.0, 2.0, ALU.is_ge, ALU.mult).then_inc(v_step, 1)
            dve.wait_ge(v_alpha, 1)
            nc.vector.tensor_scalar(valpha[:, 1, :], valpha[:, 0, :], 1.0 / HD, None, ALU.mult).then_inc(v_alpha, 1)
            dve.wait_ge(v_step, 1)
            nc.vector.tensor_scalar(vb[:], vb[:], -1.0, None, ALU.add).then_inc(v_step, 1)
            dve.wait_ge(cond_mm, 8)
            nc.vector.tensor_copy(agg_sb[0][:, 512:CW], ps_z[1][:]).then_inc(cond_dve, 1)
            nc.vector.reduce_sum(bqk_a[:], ps_s[:, 2 * S:2 * S + 4 * H].rearrange("p (a h j) -> p a h j", a=2, j=2),
                                 AX.X).then_inc(bind_dve, 1)
            nc.vector.tensor_scalar(bqk_t[:, 1], bqk, 0.0, 2.0, ALU.is_ge, ALU.mult).then_inc(bind_dve, 1)
            dve.wait_ge(bind_dve, 2)
            nc.vector.tensor_scalar(bqk_a[:], bqk_a[:], 1.0 / HD, None, ALU.mult).then_inc(bind_dve, 1)
            nc.vector.tensor_scalar(bqk_t[:, 1], bqk_t[:, 1], -1.0, None, ALU.add).then_inc(bind_dve, 1)
            dve.wait_ge(bind_dve, 4)
            nc.vector.tensor_tensor(bqk_t[:, 2].rearrange("p a (h j) -> p a h j", j=2),
                                    bqk_t[:, 1].rearrange("p a (h j) -> p a h j", j=2),
                                    bqk_a[:].unsqueeze(3).to_broadcast([P, 2, H, 2]), ALU.mult).then_inc(bind_dve, 1)
            dve.wait_ge(bind_dve, 5)
            nc.vector.tensor_tensor(bqk_t[:, 2], bqk_t[:, 2], bqk, ALU.subtract).then_inc(bind_dve, 1)
            dve.wait_ge(bind_dve, 6)
            nc.vector.tensor_tensor(bqk_t[:, 3], bqk_t[:, 2], bqk, ALU.add).then_inc(bind_dve, 1)
            dve.wait_ge(bind_dve, 7)
            nc.vector.tensor_tensor(qk[:], bqk_t[:, 3, 0, :], bqk_t[:, 3, 1, :], ALU.mult).then_inc(bind_dve, 1)
            dve.wait_ge(cond_mm, 10)
            nc.vector.tensor_copy(agg_sb[1][:, 512:CW], ps_c[1][:]).then_inc(cond_dve, 1)

            def split_a():
                dve.wait_ge(split_hi, 1)
                nc.vector.tensor_tensor(a_lo[:, Q // 2:], a_raw[:, Q // 2:], a_hi[:, Q // 2:].bitcast(F32),
                                        ALU.subtract).then_inc(split_lo, 1)

            def y_out(pair):
                n, par = number(pair), pair[1]
                wait(dve, s_mm, n)
                wait(dve, bias_in[par], pair[0] * 16 + 16)
                bias = bias_bc[par][:, :, 0, :].unsqueeze(1).to_broadcast([P, 4, 2, S])
                for j in range(2):
                    wait(dve, y_mm, n * 2 + 1 + j)
                    nc.vector.tensor_tensor(yT[:, 4 * j:4 * j + 4].rearrange("p a (b t) -> p a b t", b=2),
                                            y_banks(pair)[j][:].rearrange("p (a b t) -> p a b t", a=4, b=2),
                                            bias, ALU.add).then_inc(y_rdy, 1)

            def bias_mask(pair, j):
                par = pair[1]
                rows = slice(j * S, (j + 1) * S)
                nc.vector.tensor_tensor(bm[rows], mask_ts[rows], bias_bc[par][rows, j, 0, :],
                                        ALU.mult).then_inc(bm_rdy, 1)

            def router(a, f):
                n = number(f)
                at = lambda k: n * ROUTE + k
                scores = ps_t[:, P:P + E]
                wait(dve, rs_mm, n + 1)
                nc.vector.tensor_copy(rs[:, 0, :], scores)
                nc.vector.max(top8[:, 0, :], scores).then_inc(route, 1)
                wait(dve, route, at(1))
                nc.vector.tensor_scalar(rs[:, 3, :], scores, top8[:, 0, 0:1], None,
                                        ALU.subtract).then_inc(route, 1)
                nc.vector.match_replace(rs[:, 1, :], top8[:, 0, :], scores, LOWEST).then_inc(route, 1)
                wait(dve, route, at(3))
                if a is not None:
                    bias_mask(a, 0)
                else:
                    nc.vector.tensor_copy(gate[:, 0, 0:1], top8[:, 0, 0:1])
                nc.vector.max(top8[:, 1, :], rs[:, 1, :]).then_inc(route, 1)
                wait(dve, route, at(4))
                if a is not None:
                    bias_mask(a, 1)
                else:
                    nc.vector.tensor_copy(gate[:, 0, 0:1], top8[:, 0, 0:1])
                nc.vector.match_replace(rs[:, 2, :], top8[:, 1, :], rs[:, 1, :], LOWEST).then_inc(route, 1)
                wait(dve, route, at(5))
                nc.vector.tensor_tensor(rs[:, 5, :], rs[:, 2, :], rs[:, 0, :], ALU.not_equal).then_inc(route, 1)
                wait(dve, exp_rdy, n + 1)
                wait(dve, route, at(6))
                nc.vector.tensor_tensor(gate[:, 0, :], rs[:, 4, :], rs[:, 5, :], ALU.mult).then_inc(route, 1)
                wait(dve, route, at(7))
                nc.vector.reduce_sum(gsum[:, 0:1], gate[:, 0, :], AX.X).then_inc(route, 1)
                wait(dve, route, at(8))
                nc.vector.reciprocal(gsum[:, 1:2], gsum[:, 0:1]).then_inc(route, 1)
                wait(dve, route, at(9))
                nc.vector.tensor_scalar(gate[:, 1, :], gate[:, 0, :], gsum[:, 1:2], SCALING,
                                        ALU.mult, ALU.mult).then_inc(gate_rdy, 1)
                wait(dve, gate_rdy, n + 1)
                wait(dve, t_mm, n)
                e0 = ZW // RANK
                for lo, hi, part in ((e0, E, 1), (0, e0, 0)):
                    if part == 0:
                        wait(dve, z_mm, n * 2 + 2)
                    nc.vector.tensor_tensor(
                        zg[:, lo * RANK:hi * RANK].rearrange("p (e r) -> p e r", r=RANK),
                        z_banks(f)[part][:, 0:(hi - lo) * RANK].rearrange("p (e r) -> p e r", r=RANK),
                        gate[:, 1, lo:hi].unsqueeze(2).to_broadcast([P, hi - lo, RANK]),
                        ALU.mult).then_inc(zg_rdy, 1)

            def masked(pair):
                n = number(pair)
                wait(dve, th_rdy, n * 2 + 2)
                wait(dve, m_mm, n)
                nc.vector.scalar_tensor_tensor(out=attnT[:], in0=th[:], scalar=1.0,
                                               in1=mask_st[:].unsqueeze(1).to_broadcast([P, H, S]),
                                               op0=ALU.add, op1=ALU.mult).then_inc(attn_rdy, 1)
                wait(dve, bm_rdy, n * 2 + 2)
                nc.vector.scalar_tensor_tensor(out=cprod[:], in0=th[:], scalar=1.0,
                                               in1=bm[:].unsqueeze(1).to_broadcast([P, H, S]),
                                               op0=ALU.add, op1=ALU.mult).then_inc(c_step, 1)
                wait(dve, c_step, n * 2 + 1)
                nc.vector.reduce_sum(cvec[:], cprod[:], AX.X).then_inc(c_step, 1)

            def conv_out(pair, j):
                n, par = number(pair), pair[1]
                wait(dve, chi_rdy, n)
                wait(dve, clo_rdy, n)
                wait(dve, c_mm, n * 2 + 1 + j)
                bias = bias_bc[par][:, j, 1, :].rearrange("p (g o) -> p g o", g=G)
                nc.vector.tensor_tensor(
                    c_sb[:, :, j * S:(j + 1) * S].rearrange("p r (g o) -> p r g o", g=G),
                    ps_c[j][:].rearrange("p (g r o) -> p r g o", g=G, r=Q),
                    bias.unsqueeze(1).to_broadcast([P, Q, G, GC]), ALU.add).then_inc(c_rdy, 1)

            def m_low(pair):
                n = number(pair)
                wait(dve, m_rdy, n * 2 + 2)
                wait(dve, ax_mm, n * 2)
                for j in range(2):
                    rows = slice(j * S, (j + 1) * S)
                    nc.vector.tensor_tensor(m_lo[rows, :, rows], ps_s[rows, 0:H * S]
                                            .rearrange("p (h t) -> p h t", h=H),
                                            m_hi[rows, :, rows].bitcast(F32), ALU.subtract).then_inc(mlo_rdy, 1)

            def zt_low(pair):
                n = number(pair)
                wait(dve, zhi_rdy, n + 1)
                wait(dve, o_mm, n * 2)
                nc.vector.tensor_tensor(zt_lo[:].rearrange("p a b -> p (a b)"), ps_t[:],
                                        zt_hi[:].bitcast(F32).rearrange("p a b -> p (a b)"),
                                        ALU.subtract).then_inc(zlo_rdy, 1)

            def attn_out(pair):
                n = number(pair)
                wait(dve, c_step, n * 2 + 2)
                for h in range(H):
                    if h % 2 == 0:
                        wait(dve, ax_mm, n * 2 + 1 + h // 2)
                    nc.vector.scalar_tensor_tensor(
                        out=r_sb[:, h, :], in0=ps_y[h // 2][:, (h % 2) * HD:(h % 2 + 1) * HD],
                        scalar=cvec[:, h:h + 1], in1=vb[:, h, :], op0=ALU.add, op1=ALU.mult).then_inc(r_rdy, 1)

            def residual(pair):
                n, par = number(pair), pair[1]
                wait(dve, r_rdy, n * 4 + 4)
                for j in range(2):
                    wait(dve, o_rdy, n * 2 - 3 + j)
                    ph = slice(4 * j, 4 * j + 4)
                    by_phase = lambda t: t[:].rearrange("p h (q m) -> p q h m", q=Q)[:, ph]
                    nc.vector.tensor_tensor(
                        x1_sb[par][:, ph, j:j + M].rearrange("p q (h m) -> p q h m", h=H),
                        by_phase(r_sb), by_phase(x_sb[par]), ALU.add).then_inc(x1_rdy, 1)

            def final(pair, j):
                n, par = number(pair), pair[1]
                wait(dve, o_mm, n * 2 + 1 + j)
                wait(dve, o_out[j], n * 16)
                nc.vector.tensor_tensor(o_sb[:, j, :].rearrange("p (q m) -> p q m", q=4),
                                        ps_z[j][:].rearrange("p (q m) -> p q m", q=4),
                                        x1_sb[par][:, 4 * j:4 * j + 4, j:j + M], ALU.add).then_inc(o_rdy, 1)

            def step(a, c, f):
                if f is not None and not is_first(f) and not is_last(f):
                    final((f[0], 0) if f[1] else (f[0] - 1, 1), 1)
                if is_first(c):
                    dve.wait_ge(consts, 2)
                if c is not None:
                    residual(c)
                if a is not None and not is_second(a):
                    y_out(a)
                if is_first(f):
                    dve.wait_ge(split_hi, 2)
                    nc.vector.tensor_tensor(b_lo[:, NT // 2:], b_raw[:, NT // 2:], b_hi[:, NT // 2:].bitcast(F32),
                                            ALU.subtract).then_inc(split_lo, 1)
                if f is not None:
                    router(a, f)
                elif a is not None:
                    bias_mask(a, 0)
                    bias_mask(a, 1)
                if is_last(f):
                    final((f[0], 0), 1)
                if a is not None:
                    masked(a)
                if is_first(a):
                    y_out((0, 1))
                    dve.wait_ge(consts, 2)
                if c is not None and not is_first(c):
                    conv_out(c, 0)
                if a is not None:
                    m_low(a)
                if f is not None:
                    zt_low(f)
                if c is not None and not is_first(c):
                    conv_out(c, 1)
                if is_first(a):
                    dve.wait_ge(v_step, 5)
                if a is not None:
                    attn_out(a)
                if is_first(c):
                    split_a()
                    dve.wait_ge(scratch_out, 2 * CH * 16)
                    dve.wait_ge(wt_in[1], 32)
                    dve.wait_ge(wn_in[1], 32)
                    conv_out(c, 0)
                    conv_out(c, 1)
                if f is not None:
                    final(f, 0)

            run(dve, step)
            final((PAIRS // 2 - 1, 1), 1)

        @block.tensor
        def _(pe):
            emb = pp[:, cp["emb_t"]]
            pe.wait_ge(pp_in, 16)
            nc.tensor.matmul(ps_y[0][:, 0:B], pp[:, cp["w0"]], emb, start=True, stop=True).then_inc(cond_mm, 1)
            pe.wait_ge(cond_act, 1)
            nc.tensor.matmul(ps_y[1][:, 0:B], pp[:, cp["w1"]], h0[:], start=True, stop=True).then_inc(cond_mm, 1)
            pe.wait_ge(cond_act, 2)
            nc.tensor.matmul(ps_c[0][0:B, 0:NK], h1[:], pp[:, cp["w2"]], start=True, stop=True).then_inc(cond_mm, 1)
            pe.wait_ge(cond_dve, 5)
            pe.wait_ge(const_step, 6)
            nc.tensor.matmul(ps_c[1][0:CH * NK, 0:B], att_rep[:].rearrange("b c k -> b (c k)"),
                             ident[0:B, 0:B], start=True, stop=True).then_inc(cond_mm, 1)
            pe.wait_ge(pm_in, 16)
            pe.wait_ge(const_step, 10)
            pe.wait_ge(qk_abs, 1)
            nc.tensor.matmul(ps_s[:, 2 * S:2 * S + 4 * H], ones[:], bqk_t[:, 0].rearrange("p a t -> p (a t)"),
                             start=True, stop=True).then_inc(bind_mm, 1)
            pe.wait_ge(cond_dve, 6)
            nc.tensor.matmul(ps_s[0:B, 0:S], att4[0:NK, 0, :], pm[0:NK, cm["bias_k"]],
                             start=True, stop=True).then_inc(cond_mm, 1)
            nc.tensor.matmul(ps_s[0:B, S:2 * S], emb, pp[:, cp["cw_t"]], start=True, stop=True).then_inc(cond_mm, 1)
            for form, bank in (("wk_t", ps_z), ("wk_n", ps_c)):
                for j in range(2):
                    at = cm[form].start + j * 512
                    nc.tensor.matmul(bank[j][:], att4[:].rearrange("r c b -> r (c b)"),
                                     pm[:, at:at + 512], start=True, stop=True).then_inc(cond_mm, 1)

            def y_product(pair):
                n, par = number(pair), pair[1]
                wait(pe, x_in[par], pair[0] * 16 + 16)
                wait(pe, wt_in[par], pair[0] * 32 + 32)
                for j in range(2):
                    if not is_second(pair):
                        wait(pe, r_rdy, n * 4 - 2 + 2 * j)
                    else:
                        pe.wait_ge(cond_dve, 9)
                        pe.wait_ge(cond_act, 4)
                    for k in range(4):
                        h, half = 2 * j + k // 2, k % 2
                        last = nc.tensor.matmul(y_banks(pair)[j][:, k * P:(k + 1) * P],
                                                x_sb[par][:, h, half * P:(half + 1) * P],
                                                wt_sb[par][:], start=True, stop=True)
                    last.then_inc(y_mm, 1)

            def scores(pair):
                n = number(pair)
                wait(pe, mlo_rdy, n * 2)
                for h in range(H):
                    if h % 2 == 0:
                        wait(pe, k_rdy, n * 2 + 1 + h // 2)
                    for k in range(2):
                        last = nc.tensor.matmul(ps_s[:, h * P:(h + 1) * P], kT[:, 2 * h + k, :],
                                                yT[:, 2 * h + k, :], start=(k == 0), stop=(k == 1))
                last.then_inc(s_mm, 1)

            def m_product(pair):
                n, par = number(pair), pair[1]
                wait(pe, wn_in[par], pair[0] * 32 + 32)
                wait(pe, attn_rdy, n + 1)
                nc.tensor.matmul(ps_s[:, 0:H * S], wn_sb[par][:], attnT[:].rearrange("p h t -> p (h t)"),
                                 start=True, stop=True).then_inc(m_mm, 1)

            def attn_x(pair):
                n = number(pair)
                wait(pe, xlo_rdy, n + 1)
                wait(pe, m_rdy, n * 2 + 2)
                for h in range(H):
                    for i, (w, m) in enumerate(((m_hi, x_hi), (m_hi, x_lo), (m_lo, x_hi))):
                        if h == 0 and i == 2:
                            wait(pe, mlo_rdy, n * 2 + 2)
                        last = nc.tensor.matmul(ps_y[h // 2][:, (h % 2) * HD:(h % 2 + 1) * HD], w[:, h, :],
                                                m[:, h, :], start=(i == 0), stop=(i == 2))
                    if h % 2:
                        last.then_inc(ax_mm, 1)

            def conv(pair, first, end):
                n = number(pair)
                for jg in range(first, end):
                    j, g = jg // G, jg % G
                    wait(pe, xg_in[jg], n * 16 + 16)
                    if g == 0:
                        wait(pe, c_rdy, n * 2 - 1 + j)
                    for k in range(2):
                        last = nc.tensor.matmul(ps_c[j][:, g * P:(g + 1) * P], xg[:, j, g, k:k + M],
                                                toep_sb[:, g, k, :], start=(k == 0), stop=(k == 1))
                    if g == G - 1:
                        last.then_inc(c_mm, 1)

            def z_product(pair):
                n = number(pair)
                wait(pe, chi_rdy, n + 1)
                for part in (1, 0):
                    if is_last(pair):
                        pe.wait_ge(r_rdy, 4 * PAIRS)
                    else:
                        wait(pe, o_rdy, n * 2 - part)
                    cols = slice(part * ZW, (part + 1) * ZW)
                    bank = z_banks(pair)[part][:, 0:ZW]
                    for q in range(Q):
                        nc.tensor.matmul(bank, c_hi[:, q, :], a_hi[:, q, cols], start=(q == 0), stop=False)
                        nc.tensor.matmul(bank, c_hi[:, q, :], a_lo[:, q, cols], start=False, stop=False)
                        if part == 0 and q == ROUTER_AT[0]:
                            wait(pe, q_rdy, n + 1)
                            wait(pe, zlo_rdy, n)
                            nc.tensor.transpose(ps_t[0:RD, 0:P], q_sb[:], ident[:]).then_inc(q_mm, 1)
                        if part == 0 and q == ROUTER_AT[1]:
                            wait(pe, qT_rdy, n + 1)
                            nc.tensor.matmul(ps_t[:, P:P + E], qT_sb[:], pm[0:RD, cm["keys_t"]],
                                             start=True, stop=True).then_inc(rs_mm, 1)
                    if part == 1:
                        wait(pe, clo_rdy, n + 1)
                    for q in range(Q):
                        last = nc.tensor.matmul(bank, c_lo[:, q, :], a_hi[:, q, cols],
                                                start=False, stop=(q == Q - 1))
                    last.then_inc(z_mm, 1)

            def turn(pair):
                n = number(pair)
                wait(pe, zg_rdy, n * 2 + 2)
                for k in range(NT):
                    last = nc.tensor.transpose(ps_t[:, k * P:(k + 1) * P], zg[:, k * P:(k + 1) * P], ident[:])
                last.then_inc(t_mm, 1)

            def out_product(pair, j):
                n = number(pair)
                cols = slice(j * 512, (j + 1) * 512)
                if is_last(pair):
                    pe.wait_ge(o_rdy, n * 2 - 1 + j)
                if j == 0:
                    wait(pe, zhi_rdy, n + 1)
                for k in range(NT):
                    nc.tensor.matmul(ps_z[j][:], zt_hi[:, k, :], b_hi[:, k, cols], start=(k == 0), stop=False)
                    nc.tensor.matmul(ps_z[j][:], zt_hi[:, k, :], b_lo[:, k, cols], start=False, stop=False)
                if j == 0:
                    wait(pe, zlo_rdy, n + 1)
                for k in range(NT):
                    last = nc.tensor.matmul(ps_z[j][:], zt_lo[:, k, :], b_hi[:, k, cols],
                                            start=False, stop=(k == NT - 1))
                last.then_inc(o_mm, 1)

            def keep_busy(products):
                for _ in range(products):
                    nc.tensor.matmul(ps_t[:, 0:P], ones[:], ones[:], start=True, stop=True)

            def step(a, c, f):
                if a is not None and not is_second(a):
                    y_product(a)
                if is_first(f):
                    pe.wait_ge(split_lo_pool, 1)
                    pe.wait_ge(split_lo, 1)
                if f is not None:
                    z_product(f)
                if is_last(f):
                    out_product((f[0], 0), 1)
                if a is not None:
                    scores(a)
                if is_first(a):
                    y_product((0, 1))
                if c is not None and not is_first(c):
                    conv(c, 0, G)
                if is_second(a):
                    keep_busy(FILL[0])
                if a is not None:
                    m_product(a)
                if is_second(a):
                    keep_busy(FILL[1])
                if f is not None:
                    turn(f)
                if c is not None and not is_first(c):
                    conv(c, G, 2 * G)
                if is_first(a):
                    pe.wait_ge(consts, 2)
                if a is not None:
                    attn_x(a)
                if is_first(c):
                    pe.wait_ge(toep_in, 16)
                    conv(c, 0, 2 * G)
                if is_first(f):
                    pe.wait_ge(split_lo_pool, 2)
                    pe.wait_ge(split_lo, 2)
                if f is not None:
                    out_product(f, 0)
                if f is not None and (a is not None or is_last(f)):
                    out_product(f, 1)

            run(pe, step)


def kernel(**inputs):
    import numpy as np
    import concourse.bacc as bacc
    from concourse.bass_utils import run_bass_kernel_spmd

    inp = {k: np.asarray(v) for k, v in inputs.items()}
    x = inp["x"].reshape(B * S, H, HM, Q).transpose(0, 1, 3, 2).reshape(B * S, D)
    wk = inp["L0_cond_weight"][..., 0]

    def chunks(w):
        return w.reshape(NK, CH, CW).transpose(1, 0, 2).reshape(CH * NK, CW)

    def tile_columns(w):
        return w.reshape(H, HM, 2, 4).transpose(3, 1, 0, 2).reshape(P, 2 * H)

    w = inp["L0_cond2_weight"].reshape(G, GC, GC, TAPS)
    toep = np.zeros((GC, Q, G, 2, Q, GC), w.dtype)
    for q in range(Q):
        p = q + PAD if q < PAD else q - PAD
        for k in range(2):
            for r in range(Q):
                tap = p + Q * k - r
                if 0 <= tap < TAPS:
                    toep[:, q, :, k, r, :] = w[:, :, :, tap].transpose(2, 0, 1)
    small = {
        "emb_t": inp["cond_128"].T,
        "w0": inp["L0_cond_W0"], "b0": inp["L0_cond_b0"].reshape(P, 1),
        "w1": inp["L0_cond_W1"], "b1": inp["L0_cond_b1"].reshape(P, 1),
        "w2": inp["L0_cond_W2"], "b2": np.broadcast_to(inp["L0_cond_b2"], (B, NK)),
        "wk_n": chunks(wk.reshape(NK, S * S)),
        "wk_t": chunks(wk.transpose(0, 2, 1).reshape(NK, S * S)),
        "bias_k": inp["L0_cond_bias_k"],
        "bq": tile_columns(inp["L0_attn_bv_q"]),
        "bk": tile_columns(inp["L0_attn_bv_k"]),
        "cw_t": inp["L0_cond2_c_weight"].T,
        "fside": np.broadcast_to(inp["fside_S_0"], (B, S)),
        "keys_t": inp["L0_ffn_keys"].T,
    }

    def pack(names, rows):
        packed = np.zeros((rows, sum(names.values())), np.float32)
        for name, cols in columns(names).items():
            packed[:small[name].shape[0], cols] = small[name]
        return packed

    arrays = {
        "x": x,
        "pack_p": pack(PACK_P, P),
        "pack_m": pack(PACK_M, CH * NK),
        "bv": inp["L0_attn_bv_v"].reshape(H, HM, Q).transpose(0, 2, 1).reshape(1, D),
        "toep": toep.reshape(P, G, 2, P),
        "a_t": np.concatenate([inp["L0_ffn_A_w"].T, inp["L0_ffn_Wq_w"].T], 1).reshape(M, Q, NB + RD),
        "b_t": inp["L0_ffn_B_w"].T.reshape(NT, P, M, Q).transpose(1, 0, 3, 2).reshape(P, NT, D),
    }
    arrays = {f"in_{k}": np.ascontiguousarray(v) for k, v in arrays.items()}
    nc = bacc.Bacc("TRN2", target_bir_lowering=False, num_devices=1)
    args = [nc.dram_tensor(k, v.shape, F32, kind="ExternalInput").ap() for k, v in arrays.items()]
    out = nc.dram_tensor("out", (B * S, D), F32, kind="ExternalOutput").ap()
    adaln_attn_ffn_kernel(nc, *args, out)
    r = run_bass_kernel_spmd(nc, [arrays], core_ids=[0])
    got = r.results[0]["out"]
    return got.reshape(B, S, Q, M).transpose(0, 1, 3, 2).reshape(B, S, D)
```
